# Optimizing a Trainium2 kernel written in Bass

```python
import numpy as np
import jax
import jax.numpy as jnp

def _softmax(x, axis=-1):
    return jax.nn.softmax(x, axis=axis)

def _gelu(x):
    return jax.nn.gelu(x, approximate=True)

def _silu(x):
    return jax.nn.silu(x)

def _sigmoid(x):
    return jax.nn.sigmoid(x)

def _layernorm(x, axis=-1, eps=1e-05):
    m = jnp.mean(x, axis=axis, keepdims=True)
    v = jnp.var(x, axis=axis, keepdims=True)
    return (x - m) / jnp.sqrt(v + eps)

def _scatter_add(tgt, idx, src, axis=0):
    return tgt.at[idx].add(src)

def _segment_sum(src, seg, n):
    return jax.ops.segment_sum(src, seg, n)
kernel_name = 'mk_recurrent_d2_jaxref_r8_6a5178'

def setup_inputs(seed: int=0):
    np.random.seed(seed)
    _w = jnp.asarray

    def _L0_attn_setup():
        import jax, jax.numpy as jnp
        import numpy as np
        import math
        B, T, C = (32, 32, 128)
        LAYER_ID, NUM_LAYERS = (12, 24)
        NEG_INF = -1e+38

        def wkv(time_decay, time_first, k, v):
            w = -jnp.exp(time_decay)
            u = time_first
            kT = jnp.swapaxes(k, 0, 1)
            vT = jnp.swapaxes(v, 0, 1)

            def step(carry, kv):
                p, q, o = carry
                kt, vt = kv
                no = jnp.maximum(o, u + kt)
                A = jnp.exp(o - no)
                Bc = jnp.exp(u + kt - no)
                y = (A * p + Bc * vt) / (A * q + Bc)
                no2 = jnp.maximum(w + o, kt)
                A2 = jnp.exp(w + o - no2)
                B2 = jnp.exp(kt - no2)
                return ((A2 * p + B2 * vt, A2 * q + B2, no2), y)
            init = (jnp.zeros((k.shape[0], k.shape[2]), k.dtype), jnp.zeros((k.shape[0], k.shape[2]), k.dtype), jnp.full((k.shape[0], k.shape[2]), NEG_INF, k.dtype))
            _, yT = jax.lax.scan(step, init, (kT, vT))
            return jnp.swapaxes(yT, 0, 1)
        key = jax.random.key(seed)
        ks = jax.random.split(key, 5)
        x = jax.random.normal(ks[0], (B, T, C), dtype=jnp.float32)
        r01 = LAYER_ID / (NUM_LAYERS - 1)
        r10 = 1.0 - LAYER_ID / NUM_LAYERS
        h = jnp.arange(C, dtype=jnp.float32)
        time_decay = -5.0 + 8.0 * (h / (C - 1)) ** (0.7 + 1.3 * r01)
        tf = (jnp.arange(C) + 1) % 3 - 1
        time_first = jnp.full((C,), math.log(0.3), jnp.float32) + 0.5 * tf.astype(jnp.float32)
        xr = (jnp.arange(C, dtype=jnp.float32) / C)[None, None, :]
        time_mix_k = xr ** r10
        time_mix_v = xr ** r10 + 0.3 * r01
        time_mix_r = xr ** (0.5 * r10)
        s = 1.0 / math.sqrt(C)
        Wk = jax.random.normal(ks[1], (C, C), jnp.float32) * s
        Wv = jax.random.normal(ks[2], (C, C), jnp.float32) * s
        Wr = jax.random.normal(ks[3], (C, C), jnp.float32) * s
        Wo = jax.random.normal(ks[4], (C, C), jnp.float32) * s
        return {'x': x, 'time_decay': time_decay, 'time_first': time_first, 'time_mix_k': time_mix_k, 'time_mix_v': time_mix_v, 'time_mix_r': time_mix_r, 'Wk': Wk, 'Wv': Wv, 'Wr': Wr, 'Wo': Wo}
    _L0_attn_in = _L0_attn_setup()

    def _L0_ffn_setup():
        import jax, jax.numpy as jnp
        import numpy as np
        D = 128
        H = 16
        FF = 512
        E = 8
        K = 2
        EH = 128
        B, S = (2, 256)
        EPS = 1e-05

        def rmsnorm(x, w):
            v = jnp.mean(jnp.square(x), axis=-1, keepdims=True)
            return x * jax.lax.rsqrt(v + EPS) * w

        def _dense_path(x, wq, wk, wv, wo, w1, w2, w3, attn_norm_w, ff_norm_w):
            b, s, d = x.shape
            hd = d // H
            q = (x @ wq).reshape(b, s, H, hd)
            k = (x @ wk).reshape(b, s, H, hd)
            v = (x @ wv).reshape(b, s, H, hd)
            scores = jnp.einsum('bqhd,bkhd->bhqk', q, k) / np.sqrt(hd).astype(np.float32)
            causal = jnp.tril(jnp.ones((s, s), bool))
            scores = jnp.where(causal, scores, jnp.finfo(scores.dtype).min)
            attn = jax.nn.softmax(scores, axis=-1)
            o = jnp.einsum('bhqk,bkhd->bqhd', attn, v).reshape(b, s, d)
            h = x + rmsnorm(o @ wo, attn_norm_w)
            ffn = jax.nn.silu(h @ w1) * (h @ w3) @ w2
            return h + rmsnorm(ffn, ff_norm_w)

        def _sparse_path(x, router_w, ew1, ew2, ew3, moe_norm_w):
            b, s, d = x.shape
            xt = x.reshape(-1, d)
            probs = jax.nn.softmax(xt @ router_w, axis=-1)
            topw, topi = jax.lax.top_k(probs, K)
            g = jax.nn.silu(jnp.einsum('td,edh->eth', xt, ew1)) * jnp.einsum('td,edh->eth', xt, ew3)
            eo = jnp.einsum('eth,ehd->ted', g, ew2)
            sel = jnp.take_along_axis(eo, topi[:, :, None], axis=1)
            moe_out = jnp.sum(topw[:, :, None] * sel, axis=1).reshape(b, s, d)
            return rmsnorm(moe_out, moe_norm_w)
        key = jax.random.key(seed)
        ks = jax.random.split(key, 16)
        s = 0.02
        return {'x': jax.random.normal(ks[0], (B, S, D), jnp.float32), 'wq': jax.random.normal(ks[1], (D, D), jnp.float32) * s, 'wk': jax.random.normal(ks[2], (D, D), jnp.float32) * s, 'wv': jax.random.normal(ks[3], (D, D), jnp.float32) * s, 'wo': jax.random.normal(ks[4], (D, D), jnp.float32) * s, 'w1': jax.random.normal(ks[5], (D, FF), jnp.float32) * s, 'w2': jax.random.normal(ks[6], (FF, D), jnp.float32) * s, 'w3': jax.random.normal(ks[7], (D, FF), jnp.float32) * s, 'attn_norm_w': jnp.ones((D,), jnp.float32), 'ff_norm_w': jnp.ones((D,), jnp.float32), 'moe_norm_w': jnp.ones((D,), jnp.float32), 'router_w': jax.random.normal(ks[8], (D, E), jnp.float32) * s, 'ew1': jax.random.normal(ks[9], (E, D, EH), jnp.float32) * s, 'ew2': jax.random.normal(ks[10], (E, EH, D), jnp.float32) * s, 'ew3': jax.random.normal(ks[11], (E, D, EH), jnp.float32) * s}
    _L0_ffn_in = _L0_ffn_setup()

    def _L1_attn_setup():
        import jax, jax.numpy as jnp
        import numpy as np
        import itertools
        B, T, C, H = (2, 256, 128, 8)
        HD = C // H

        def _head_dirs():
            signs = [-1.0, 1.0]
            tri = np.array(list(itertools.product(signs, repeat=3)), dtype=np.float32)
            tri = tri / np.linalg.norm(tri, axis=1, keepdims=True)
            return jnp.asarray(tri[:H])
        key = jax.random.key(seed)
        ks = jax.random.split(key, 5)
        w = lambda k, sh: jax.random.normal(k, sh, dtype=jnp.float32) * 0.02
        return {'x': jax.random.normal(ks[0], (B, T, C), dtype=jnp.float32), 'Wq': w(ks[1], (H * 3, C)), 'Wk': w(ks[2], (H * 3, C)), 'Wv': w(ks[3], (C, C)), 'Wo': w(ks[4], (C, C)), 'scale': jnp.asarray(1.0 / np.sqrt(3.0), dtype=jnp.float32)}
    _L1_attn_in = _L1_attn_setup()

    def _L1_ffn_setup():
        import math
        import jax, jax.numpy as jnp
        from jax import lax
        import numpy as np
        E = 16
        K = 2
        CF = 1.25
        key = jax.random.key(seed)
        k0, k1, k2, k3, k4 = jax.random.split(key, 5)
        B, S, D, H = (2, 256, 128, 128)
        scale = 0.02
        return {'x': jax.random.normal(k0, (B, S, D), dtype=jnp.float32), 'router_w': jax.random.normal(k1, (D, E), dtype=jnp.float32) * scale, 'gate_w': jax.random.normal(k2, (E, D, H), dtype=jnp.float32) * scale, 'up_w': jax.random.normal(k3, (E, D, H), dtype=jnp.float32) * scale, 'down_w': jax.random.normal(k4, (E, H, D), dtype=jnp.float32) * scale}
    _L1_ffn_in = _L1_ffn_setup()
    _d = {'L0_attn_x': _L0_attn_in['x'], 'L0_attn_time_decay': _L0_attn_in['time_decay'], 'L0_attn_time_first': _L0_attn_in['time_first'], 'L0_attn_time_mix_k': _L0_attn_in['time_mix_k'], 'L0_attn_time_mix_v': _L0_attn_in['time_mix_v'], 'L0_attn_time_mix_r': _L0_attn_in['time_mix_r'], 'L0_attn_Wk': _L0_attn_in['Wk'], 'L0_attn_Wv': _L0_attn_in['Wv'], 'L0_attn_Wr': _L0_attn_in['Wr'], 'L0_attn_Wo': _L0_attn_in['Wo'], 'L0_ffn_wq': _L0_ffn_in['wq'], 'L0_ffn_wk': _L0_ffn_in['wk'], 'L0_ffn_wv': _L0_ffn_in['wv'], 'L0_ffn_wo': _L0_ffn_in['wo'], 'L0_ffn_w1': _L0_ffn_in['w1'], 'L0_ffn_w2': _L0_ffn_in['w2'], 'L0_ffn_w3': _L0_ffn_in['w3'], 'L0_ffn_attn_norm_w': _L0_ffn_in['attn_norm_w'], 'L0_ffn_ff_norm_w': _L0_ffn_in['ff_norm_w'], 'L0_ffn_moe_norm_w': _L0_ffn_in['moe_norm_w'], 'L0_ffn_router_w': _L0_ffn_in['router_w'], 'L0_ffn_ew1': _L0_ffn_in['ew1'], 'L0_ffn_ew2': _L0_ffn_in['ew2'], 'L0_ffn_ew3': _L0_ffn_in['ew3'], 'L1_attn_Wq': _L1_attn_in['Wq'], 'L1_attn_Wk': _L1_attn_in['Wk'], 'L1_attn_Wv': _L1_attn_in['Wv'], 'L1_attn_Wo': _L1_attn_in['Wo'], 'L1_attn_scale': _L1_attn_in['scale'], 'L1_ffn_router_w': _L1_ffn_in['router_w'], 'L1_ffn_gate_w': _L1_ffn_in['gate_w'], 'L1_ffn_up_w': _L1_ffn_in['up_w'], 'L1_ffn_down_w': _L1_ffn_in['down_w']}
    _x0 = _d['L0_attn_x']
    _d['L0_attn_x'] = jax.random.normal(jax.random.fold_in(jax.random.key(seed), 1), (16, 512, 128), dtype=_x0.dtype)
    del _x0
    return _d

def reference(L0_attn_x, L0_attn_time_decay, L0_attn_time_first, L0_attn_time_mix_k, L0_attn_time_mix_v, L0_attn_time_mix_r, L0_attn_Wk, L0_attn_Wv, L0_attn_Wr, L0_attn_Wo, L0_ffn_wq, L0_ffn_wk, L0_ffn_wv, L0_ffn_wo, L0_ffn_w1, L0_ffn_w2, L0_ffn_w3, L0_ffn_attn_norm_w, L0_ffn_ff_norm_w, L0_ffn_moe_norm_w, L0_ffn_router_w, L0_ffn_ew1, L0_ffn_ew2, L0_ffn_ew3, L1_attn_Wq, L1_attn_Wk, L1_attn_Wv, L1_attn_Wo, L1_attn_scale, L1_ffn_router_w, L1_ffn_gate_w, L1_ffn_up_w, L1_ffn_down_w):

    def _L0_attn_ref(x, time_decay, time_first, time_mix_k, time_mix_v, time_mix_r, Wk, Wv, Wr, Wo):
        import jax, jax.numpy as jnp
        import numpy as np
        import math
        B, T, C = (32, 32, 128)
        LAYER_ID, NUM_LAYERS = (12, 24)
        NEG_INF = -1e+38

        def wkv(time_decay, time_first, k, v):
            w = -jnp.exp(time_decay)
            u = time_first
            kT = jnp.swapaxes(k, 0, 1)
            vT = jnp.swapaxes(v, 0, 1)

            def step(carry, kv):
                p, q, o = carry
                kt, vt = kv
                no = jnp.maximum(o, u + kt)
                A = jnp.exp(o - no)
                Bc = jnp.exp(u + kt - no)
                y = (A * p + Bc * vt) / (A * q + Bc)
                no2 = jnp.maximum(w + o, kt)
                A2 = jnp.exp(w + o - no2)
                B2 = jnp.exp(kt - no2)
                return ((A2 * p + B2 * vt, A2 * q + B2, no2), y)
            init = (jnp.zeros((k.shape[0], k.shape[2]), k.dtype), jnp.zeros((k.shape[0], k.shape[2]), k.dtype), jnp.full((k.shape[0], k.shape[2]), NEG_INF, k.dtype))
            _, yT = jax.lax.scan(step, init, (kT, vT))
            return jnp.swapaxes(yT, 0, 1)
        xx = jnp.pad(x, ((0, 0), (1, 0), (0, 0)))[:, :-1, :]
        xk = x * time_mix_k + xx * (1.0 - time_mix_k)
        xv = x * time_mix_v + xx * (1.0 - time_mix_v)
        xr = x * time_mix_r + xx * (1.0 - time_mix_r)
        k = jnp.einsum('btc,dc->btd', xk, Wk)
        v = jnp.einsum('btc,dc->btd', xv, Wv)
        r = jnp.einsum('btc,dc->btd', xr, Wr)
        sr = jax.nn.sigmoid(r)
        rwkv = sr * wkv(time_decay, time_first, k, v)
        return jnp.einsum('btc,dc->btd', rwkv, Wo)

    def _L0_ffn_ref(x, wq, wk, wv, wo, w1, w2, w3, attn_norm_w, ff_norm_w, moe_norm_w, router_w, ew1, ew2, ew3):
        import jax, jax.numpy as jnp
        import numpy as np
        D = 128
        H = 16
        FF = 512
        E = 8
        K = 2
        EH = 128
        B, S = (2, 256)
        EPS = 1e-05

        def rmsnorm(x, w):
            v = jnp.mean(jnp.square(x), axis=-1, keepdims=True)
            return x * jax.lax.rsqrt(v + EPS) * w

        def _dense_path(x, wq, wk, wv, wo, w1, w2, w3, attn_norm_w, ff_norm_w):
            b, s, d = x.shape
            hd = d // H
            q = (x @ wq).reshape(b, s, H, hd)
            k = (x @ wk).reshape(b, s, H, hd)
            v = (x @ wv).reshape(b, s, H, hd)
            scores = jnp.einsum('bqhd,bkhd->bhqk', q, k) / np.sqrt(hd).astype(np.float32)
            causal = jnp.tril(jnp.ones((s, s), bool))
            scores = jnp.where(causal, scores, jnp.finfo(scores.dtype).min)
            attn = jax.nn.softmax(scores, axis=-1)
            o = jnp.einsum('bhqk,bkhd->bqhd', attn, v).reshape(b, s, d)
            h = x + rmsnorm(o @ wo, attn_norm_w)
            ffn = jax.nn.silu(h @ w1) * (h @ w3) @ w2
            return h + rmsnorm(ffn, ff_norm_w)

        def _sparse_path(x, router_w, ew1, ew2, ew3, moe_norm_w):
            b, s, d = x.shape
            xt = x.reshape(-1, d)
            probs = jax.nn.softmax(xt @ router_w, axis=-1)
            topw, topi = jax.lax.top_k(probs, K)
            g = jax.nn.silu(jnp.einsum('td,edh->eth', xt, ew1)) * jnp.einsum('td,edh->eth', xt, ew3)
            eo = jnp.einsum('eth,ehd->ted', g, ew2)
            sel = jnp.take_along_axis(eo, topi[:, :, None], axis=1)
            moe_out = jnp.sum(topw[:, :, None] * sel, axis=1).reshape(b, s, d)
            return rmsnorm(moe_out, moe_norm_w)
        dense_out = _dense_path(x, wq, wk, wv, wo, w1, w2, w3, attn_norm_w, ff_norm_w)
        sparse_out = _sparse_path(x, router_w, ew1, ew2, ew3, moe_norm_w)
        return dense_out + sparse_out

    def _L1_attn_ref(x, Wq, Wk, Wv, Wo, scale):
        import jax, jax.numpy as jnp
        import numpy as np
        import itertools
        B, T, C, H = (2, 256, 128, 8)
        HD = C // H

        def _head_dirs():
            signs = [-1.0, 1.0]
            tri = np.array(list(itertools.product(signs, repeat=3)), dtype=np.float32)
            tri = tri / np.linalg.norm(tri, axis=1, keepdims=True)
            return jnp.asarray(tri[:H])
        Bb, Tt, Cc = x.shape
        dirs = _head_dirs()
        q3 = (x @ Wq.T).reshape(Bb, Tt, H, 3).transpose(0, 2, 1, 3)
        k3 = (x @ Wk.T).reshape(Bb, Tt, H, 3).transpose(0, 2, 1, 3)
        v = (x @ Wv.T).reshape(Bb, Tt, H, HD).transpose(0, 2, 1, 3)
        q_on_dir = jnp.einsum('bhtd,hd->bht', q3, dirs)
        k_on_dir = jnp.einsum('bhtd,hd->bht', k3, dirs)
        scores = jnp.einsum('bhtd,bhsd->bhts', q3, k3) * scale + q_on_dir[..., :, None] * k_on_dir[..., None, :]
        causal = jnp.tril(jnp.ones((Tt, Tt), dtype=bool))
        scores = jnp.where(causal, scores, -jnp.inf)
        attn = jax.nn.softmax(scores, axis=-1)
        out = jnp.einsum('bhts,bhsd->bhtd', attn, v)
        out = out.transpose(0, 2, 1, 3).reshape(Bb, Tt, Cc)
        return out @ Wo.T

    def _L1_ffn_ref(x, router_w, gate_w, up_w, down_w):
        import math
        import jax, jax.numpy as jnp
        from jax import lax
        import numpy as np
        E = 16
        K = 2
        CF = 1.25
        B, S, D = x.shape
        xf = x.reshape(-1, D)
        T = B * S
        capacity = max(1, math.ceil(T * K / E * CF))
        Cbuf = K * capacity
        logits = xf @ router_w
        probs = jax.nn.softmax(logits, axis=-1)
        w, idx = lax.top_k(probs, K)
        oh = jax.nn.one_hot(idx, E, dtype=w.dtype)
        rank = jnp.cumsum(oh, axis=0) - oh
        myrank = jnp.sum(rank * oh, axis=-1)
        keep = myrank < capacity
        w = jnp.where(keep, w, 0.0)
        flat_e = idx.reshape(-1)
        flat_w = w.reshape(-1)
        keep_f = keep.reshape(-1)
        tok = jnp.repeat(jnp.arange(T, dtype=jnp.int32), K)
        ohk = jax.nn.one_hot(flat_e, E, dtype=jnp.int32) * keep_f[:, None].astype(jnp.int32)
        pos = jnp.cumsum(ohk, axis=0) - ohk
        slot = jnp.sum(pos * ohk, axis=-1)
        e_idx = jnp.where(keep_f, flat_e, E)
        dispatch = jnp.full((E + 1, Cbuf), T, dtype=jnp.int32).at[e_idx, slot].set(tok)
        wbuf = jnp.zeros((E + 1, Cbuf), dtype=w.dtype).at[e_idx, slot].set(flat_w)
        dispatch = dispatch[:E]
        wbuf = wbuf[:E]
        x_pad = jnp.concatenate([xf, jnp.zeros((1, D), xf.dtype)], axis=0)
        xe = x_pad[dispatch]
        gate = jnp.einsum('ecd,edh->ech', xe, gate_w)
        up = jnp.einsum('ecd,edh->ech', xe, up_w)
        hidden = jax.nn.silu(gate) * up
        out = jnp.einsum('ech,ehd->ecd', hidden, down_w)
        out = out * wbuf[:, :, None]
        combined = jnp.zeros((T + 1, D), dtype=xf.dtype).at[dispatch.reshape(-1)].add(out.reshape(-1, D))
        return combined[:T].reshape(B, S, D)
    x = L0_attn_x
    xn = _layernorm(x, axis=-1)
    s = _L0_attn_ref(xn, L0_attn_time_decay, L0_attn_time_first, L0_attn_time_mix_k, L0_attn_time_mix_v, L0_attn_time_mix_r, L0_attn_Wk, L0_attn_Wv, L0_attn_Wr, L0_attn_Wo)
    g = _silu(_L0_ffn_ref(xn, L0_ffn_wq, L0_ffn_wk, L0_ffn_wv, L0_ffn_wo, L0_ffn_w1, L0_ffn_w2, L0_ffn_w3, L0_ffn_attn_norm_w, L0_ffn_ff_norm_w, L0_ffn_moe_norm_w, L0_ffn_router_w, L0_ffn_ew1, L0_ffn_ew2, L0_ffn_ew3))
    x = x + s * g
    xn = _layernorm(x, axis=-1)
    s = _L1_attn_ref(xn, L1_attn_Wq, L1_attn_Wk, L1_attn_Wv, L1_attn_Wo, L1_attn_scale)
    g = _silu(_L1_ffn_ref(xn, L1_ffn_router_w, L1_ffn_gate_w, L1_ffn_up_w, L1_ffn_down_w))
    x = x + s * g
    return x

_drawn_inputs = setup_inputs


def setup_inputs(seed=0):
    import zlib

    import numpy as np

    out = dict(_drawn_inputs(seed))
    spreads = {'L0_ffn_attn_norm_w': (1.0, 0.2),
     'L0_ffn_ff_norm_w': (1.0, 0.2),
     'L0_ffn_moe_norm_w': (1.0, 0.6)}
    factors = {'L0_ffn_wq': 3.542,
     'L0_ffn_wk': 3.364,
     'L1_attn_Wq': 8.0,
     'L1_attn_Wk': 8.0,
     'L1_attn_Wv': 8.0,
     'L1_attn_Wo': 8.0,
     'L1_ffn_router_w': 8.0,
     'L1_ffn_gate_w': 8.0,
     'L1_ffn_up_w': 8.0,
     'L1_ffn_down_w': 8.0}
    for name, (base, spread) in spreads.items():
        noise = np.random.default_rng([zlib.crc32(name.encode()), seed]).standard_normal(out[name].shape)
        drawn = base * np.exp(spread * noise) if base else spread * noise
        out[name] = jnp.asarray(drawn.astype(out[name].dtype))
    for name, factor in factors.items():
        out[name] = (out[name] * factor).astype(out[name].dtype)
    return out
```

```python
from contextlib import ExitStack

import numpy as np

import concourse.bass as bass
import concourse.mybir as mybir

F32 = mybir.dt.float32
BF16 = mybir.dt.bfloat16
ALU = mybir.AluOpType
ACT = mybir.ActivationFunctionType
AX = mybir.AxisListType

P = 128
EPS = 1e-5
NEG = -1e38

Q_RUNS = [(0, 3, 0, 0), (3, 2, 1, 0), (5, 1, 2, 0)]
K_RUNS = [(0, 3, 0, 1), (3, 2, 0, 1), (5, 1, 0, 0)]
COPIES, PARTS = 6, 3


class Slot:

    def __init__(self, tile, full, taken, uses):
        self.tile, self.full, self.taken, self.uses = tile, full, taken, list(uses)
        self.per_row = len(self.uses)

    def claim(self, pe, b, use):
        pe.wait_ge(self.taken, b * self.per_row + self.uses.index(use) + 1)

    def filled(self, eng, b, use):
        eng.wait_ge(self.full, b * self.per_row + self.uses.index(use) + 1)

    def drawn(self, eng, b, use):
        eng.wait_ge(self.taken, b * self.per_row + self.uses.index(use) + 2)


def max_units(heads):
    out = []
    for i, n in ((3, 2), (2, 2), (1, 4), (0, 8)):
        out += [(i, h, n) for h in range(0, heads, n)]
    return out


def build(nc, a, out):
    B, T, C = a["x"].shape
    NB = T // P
    H0, D0, J0 = 16, 8, 8
    H1, D1, J1 = 8, 4, 4
    G0, G1 = H0 // 4, H1 // 4
    E0, E1 = a["ew1"].shape[0], a["gate_w"].shape[0]
    FF = a["w1"].shape[1]
    NF = FF // P
    CAPACITY = float(max(1, -(-(B * T * 2 * 5) // (E1 * 4))))

    ctx = ExitStack()
    with ctx:
        def sb(name, shape, dt=F32):
            return ctx.enter_context(nc.sbuf_tensor(name, shape, dt))

        def sem(name):
            return ctx.enter_context(nc.semaphore(name))

        ident = sb("ident", [P, P])
        identb = sb("identb", [P, P], BF16)
        future_key = sb("future_key", [P, P], BF16)
        past_query = sb("past_query", [P, P], BF16)
        earlier = sb("earlier", [P, P], BF16)
        onesb = sb("onesb", [P, P], BF16)
        pick = sb("pick", [48, 16, P], BF16)
        ramp = sb("ramp", [P, NB, 16])
        m4 = sb("m4", [24, 32])
        wq, wk, wv, wo = (sb(n, [P, P]) for n in ("wq", "wk", "wv", "wo"))
        rk, rv, rr, ro = (sb(n, [P, P]) for n in ("rk", "rv", "rr", "ro"))
        w1, w3 = sb("w1", [P, FF]), sb("w3", [P, FF])
        w2 = sb("w2", [P, NF, P])
        router0, router1 = sb("router0", [P, E0]), sb("router1", [P, E1])
        ew1, ew3, ew2 = (sb(n, [P, E0, P]) for n in ("ew1", "ew3", "ew2"))
        gw, uw, dw = (sb(n, [P, E1, P]) for n in ("gw", "uw", "dw"))
        norms = sb("norms", [P, 3, C])
        cols = sb("cols", [P, 5])
        decay = sb("decay", [P, 1])
        omix = sb("omix", [P, 3])
        wqk3 = sb("wqk3", [24, 2, P])
        wqk4 = sb("wqk4", [P, 2, 32])
        v1w, o1w = sb("v1w", [P, P]), sb("o1w", [P, P])
        scale = sb("scale", [32, 1])
        scale_dims = sb("scale_dims", [32, 2])
        q_scale1 = sb("q_scale1", [32, 1])
        minus_half = sb("minus_half", [P, NB])

        x_in = sb("x_in", [P, NB, C])
        x_cur = sb("x_cur", [P, NB, C])
        stats = sb("stats", [P, NB, 6])
        meanvar = sb("meanvar", [P, NB, 2])
        rstd = sb("rstd", [P, NB])
        xn = sb("xn", [P, NB, C])
        xnT = sb("xnT", [P, 1 + T])
        QS = [sb("q_stack0", [P, J0, T], BF16), sb("q_stack1", [P, J1, T], BF16)]
        KS = [sb("k_stack0", [P, J0, T], BF16), sb("k_stack1", [P, J1, T], BF16)]
        V = [sb("v0", [P, NB, H0, 32]), sb("v1", [P, NB, H1, 32])]
        row_max = sb("row_max", [P, NB, 16])
        max_rest = sb("max_rest", [P, NB, 16])
        max_parts = sb("max_parts", [P, NB, PARTS, 16], BF16)
        maxT = sb("maxT", [48, T], BF16)
        probs = sb("probs", [P, 2, 5, 1024])
        attnU = sb("attnU", [P, 2, T])
        rsum = sb("rsum", [P, NB, 4])
        attn = sb("attn", [P, NB, C])
        attnT = sb("attnT", [P, T])
        logits = sb("logits", [P, NB, 16])
        pri = sb("pri", [P, NB, 16])
        first = sb("first", [P, NB, 2, 16])
        top = sb("top", [P, NB, 4])
        expl = sb("expl", [P, NB, 16])
        wtop = sb("wtop", [P, NB, 16])
        w_rest = sb("w_rest", [P, NB, 16])
        w_parts = sb("w_parts", [P, NB, PARTS, 16], BF16)
        weightT = sb("weightT", [48, T], BF16)
        firstb = sb("firstb", [P, NB, 2, 16], BF16)
        rank = sb("rank", [P, NB, 2, 16])
        taken = sb("taken", [P, 2, 16])
        yT = sb("yT", [P, T])
        kv = sb("kv", [P, 2, T])
        er = sb("er", [P, T])
        o_all = sb("o_all", [P, 1 + T])
        p_all = sb("p_all", [P, 1 + T])
        q_all = sb("q_all", [P, 1 + T])
        expo = sb("expo", [P, 4, T])
        bv = sb("bv", [P, T])
        t1, t2, t3 = sb("t1", [P, T]), sb("t2", [P, T]), sb("t3", [P, T])
        rwkvT = sb("rwkvT", [P, T])
        sq = sb("sq", [P, NB, C])
        ssum = sb("ssum", [P, 3, NB])
        ssum_e = sb("ssum_e", [P, NB])
        rms = sb("rms", [P, 3, NB])
        sparse = sb("sparse", [P, NB, C])
        gate = sb("gate", [P, NB, C])
        x_out = sb("x_out", [P, NB, C])

        def share(tile, col, n, pattern=None, **sizes):
            view = tile[:, col * T:(col + n) * T]
            return view.rearrange(pattern, **sizes) if pattern else view

        room = probs[:].rearrange("p g u t -> p (g u t)")
        start_room = room
        compact = share(room, 0, 2, "p (s t) -> p s t", s=2)
        split_rest = share(room, 2, 2, "p (s t) -> p s t", s=2)
        parts = room[:, 4 * T:7 * T].bitcast(BF16).rearrange("p (a s t) -> p a s t", a=2, s=PARTS)
        hidw = share(room, 7, 2, "p (s t) -> p s t", s=2)
        mix = share(room, 10, 3, "p (s t) -> p s t", s=3)
        mix_a, mix_b = share(room, 13, 1), share(room, 14, 1)
        silu = share(room, 15, 2, "p (s t) -> p s t", s=2)
        hid = share(room, 17, 2, "p (s t) -> p s t", s=2)
        room = expo[:].rearrange("p s t -> p (s t)")
        tok_a, hres, pre = (share(room, n, 1, "p (i c) -> p i c", c=C) for n in range(3))
        hT = share(room, 3, 1)

        qk_dram = nc.dram_tensor("qk_scratch", [2, PARTS, P, T], BF16, kind="Internal").ap()
        max_dram = nc.dram_tensor("max_scratch", [48, T], BF16, kind="Internal").ap()

        def stand(eng):
            eng.sem_inc(waits_met, 1)

        pair_order = [("moe0", e) for e in range(E0)]
        pair_order += [("max0", n) for n in range(len(max_units(H0)))]
        pair_order += ["rwkv_kv", "rwkv_r"]
        pair_order += [("exp0", g, u) for g in range(G0) for u in range(5)]
        pair_order += [("ffn", f) for f in range(NF)]
        pair_order += [("moe1", e) for e in range(E1)]
        pair_order += [("max1", n) for n in range(len(max_units(H1)))]
        pair_order += [("exp1", g, u) for g in range(G1) for u in range(5)]
        uses = {
            "A": ["xnT0", "router0", "weightT0", *[("w0", e) for e in range(0, E0, 2)], "maxT0",
                  *[("attnN0", g) for g in range(G0)], "o_proj0", "ffn_tok", "s0",
                  "xnT1", "router1", "rank", "weightT1", *[("w1", e) for e in range(0, E1, 2)], "maxT1",
                  *[("attnN1", g) for g in range(G1)], "s1"],
            "B": ["q0", *[("w0", e) for e in range(1, E0, 2)], "moe0_tok", "attnT0", "hT",
                  "q1", *[("w1", e) for e in range(1, E1, 2)], "moe1_tok", "attnT1"],
            "C": ["k0", "moe0_sum", "ffn_sum", "k1", "moe1_sum"],
            "O": ["v0", *[("pv0", g) for g in range(G0)], "v1", *[("pv1", g) for g in range(G1)]],
        }

        def psum(name, shape):
            return ctx.enter_context(nc.psum_tensor(name, shape, F32))

        pairs = [Slot(psum(f"pair{i}", [P, 2, T]), sem(f"pair{i}_full"), sem(f"pair{i}_taken"), pair_order[i::2])
                 for i in range(2)]
        A, BK, CK, O = (Slot(psum(f"bank{n}", [P, T]), sem(f"bank{n}_full"), sem(f"bank{n}_taken"), uses[n])
                        for n in "ABCO")

        def pair_of(use):
            return pairs[pair_order.index(use) % 2]

        weights_loaded = sem("weights_loaded")
        direction_product = sem("direction_product")
        decay_exp = sem("decay_exp")
        setup_done = sem("setup_done")
        v_cleared = sem("v_cleared")
        x_loaded = sem("x_loaded")
        x_in_free = sem("x_in_free")
        var_ready = sem("var_ready")
        rstd_ready = sem("rstd_ready")
        xn_ready = sem("xn_ready")
        parts_ready = sem("parts_ready")
        parts_stored = sem("parts_stored")
        stacks_loaded = sem("stacks_loaded")
        max_parts_ready = sem("max_parts_ready")
        max_stored = sem("max_stored")
        max_loaded = sem("max_loaded")
        attn_ready = sem("attn_ready")
        logits_shifted = sem("logits_shifted")
        expl_ready = sem("expl_ready")
        choice_ready = sem("choice_ready")
        w_parts_ready = sem("w_parts_ready")
        silu_ready = sem("silu_ready")
        hid_used = sem("hid_used")
        sumsq_ready = sem("sumsq_ready")
        rms_ready = sem("rms_ready")
        h_ready = sem("h_ready")
        mix_ready = sem("mix_ready")
        expo_args = sem("expo_args")
        expo_ready = sem("expo_ready")
        rwkv_ready = sem("rwkv_ready")
        pre_ready = sem("pre_ready")
        gate_ready = sem("gate_ready")
        out_ready = sem("out_ready")
        out_stored = sem("out_stored")
        dve_step = sem("dve_step")
        pool_step = sem("pool_step")
        waits_met = sem("waits_met")
        UNITS = E0 + NF + E1
        HID_WAITS = UNITS - 3
        DVE_STEPS, POOL_STEPS = 77, 8

        loads = []

        def load(dst, src):
            loads.append((dst, src))

        narrow = [(future_key[:], share(start_room, 0, 1)[:, 0:P]), (past_query[:], share(start_room, 1, 1)[:, 0:P]),
                  (earlier[:], share(start_room, 2, 1)[:, 0:P]),
                  (pick[:].rearrange("p e n -> p (e n)"), share(start_room, 3, 4)[0:48])]
        for (_, wide), src in zip(narrow, ("future_key", "past_query", "earlier", "pick")):
            load(wide, a[src])
        for dst, src in ((ident, "ident"), (ramp, "ramp"), (m4, "m4"),
                         (scale_dims, "scale_dims"),
                         (wq, "wq"), (wk, "wk"), (wv, "wv"), (wo, "wo"), (rk, "rk"), (rv, "rv"), (rr, "rr"), (ro, "ro"),
                         (w1, "w1"), (w3, "w3"), (router0, "router0"), (router1, "router1"), (v1w, "v1w"), (o1w, "o1w")):
            load(dst[:], a[src])
        load(w2[:], a["w2"].rearrange("(f p) d -> p f d", p=P))
        for dst, src in ((ew1, "ew1"), (ew3, "ew3"), (ew2, "ew2"), (gw, "gate_w"), (uw, "up_w"), (dw, "down_w")):
            load(dst[:], a[src].rearrange("e p h -> p e h"))
        for n, src in enumerate(("attn_norm_w", "ff_norm_w", "moe_norm_w")):
            load(norms[:, n, :], a[src].rearrange("(o c) -> o c", o=1).to_broadcast([P, C]))
        for n, src in enumerate(("time_decay", "time_first", "time_mix_k", "time_mix_v", "time_mix_r")):
            load(cols[:, n:n + 1], a[src].rearrange("(c o) -> c o", o=1))
        load(wqk3[:, 0, :], a["Wq1"])
        load(wqk3[:, 1, :], a["Wk1"])
        load(scale[:], a["scale"].to_broadcast([32, 1]))

        x_rows = a["x"].rearrange("b (i p) c -> b p i c", p=P)
        out_rows = out.rearrange("b (i p) c -> b p i c", p=P)

        block = ctx.enter_context(nc.Block())

        @block.sync
        def _(sp):
            for dst, src in loads:
                sp.dma_start(dst, src).then_inc(weights_loaded, 16)
            with sp.Fori(0, B) as b:
                sp.wait_ge(x_in_free, b + 1)
                sp.dma_start(x_in[:], x_rows[b]).then_inc(x_loaded, 16)
                for layer, (D, J) in enumerate(((D0, J0), (D1, J1))):
                    rows = 2 * D * J
                    Q, K = QS[layer], KS[layer]
                    sp.wait_ge(parts_ready, b * 2 + layer + 1)
                    for t in range(2):
                        sp.dma_start(qk_dram[t, :, 0:rows, :].rearrange("s p t -> p s t"),
                                     parts[0:rows, t]).then_inc(parts_stored, 16)
                    sp.wait_ge(parts_stored, b * 64 + layer * 32 + 32)
                    for t, (stack, runs) in enumerate(((Q, Q_RUNS), (K, K_RUNS))):
                        for half in range(2):
                            for c0, n, part, step in runs:
                                src = qk_dram[t, part:part + (n if step else 1), half * D * J:(half + 1) * D * J, :]
                                src = src.rearrange("s (d j) t -> s d (j t)", d=D)
                                if not step and n > 1:
                                    src = src.to_broadcast([n, D, J * T])
                                p0 = 64 * half + c0 * D
                                sp.dma_start(stack[p0:p0 + n * D].rearrange("p j t -> p (j t)"), src)\
                                    .then_inc(stacks_loaded, 16)
                    A.drawn(sp, b, f"maxT{layer}")
                    sp.dma_start(max_dram, maxT[:]).then_inc(max_stored, 16)
                    sp.wait_ge(max_stored, b * 32 + layer * 16 + 16)
                    for half in range(2):
                        p0 = 64 * half + COPIES * D
                        src = max_dram.rearrange("(s h) t -> s h t", s=PARTS)[:, half * J:(half + 1) * J, :]
                        sp.dma_start(Q[p0:p0 + PARTS], src).then_inc(max_loaded, 16)

        @block.tensor
        def _(pe):
            pe.wait_ge(weights_loaded, 16 * len(loads))
            for t in range(2):
                mm = pe.matmul(BK.tile[:, 32 * t:32 * t + 32], wqk3[:, t, :], m4[:], start=True, stop=True)
            mm.then_inc(direction_product, 1)
            pe.wait_ge(setup_done, 1)

            with pe.Fori(0, B) as b:
                def transpose_blocks(slot, use, src):
                    slot.claim(pe, b, use)
                    for i in range(NB):
                        mm = pe.transpose(slot.tile[:, i * P:(i + 1) * P], src(i), ident[:])
                    mm.then_inc(slot.full, 1)

                def parts_to_rows(slot, use, src):
                    slot.claim(pe, b, use)
                    stand(pe)
                    dst = slot.tile[:].bitcast(BF16)
                    for i in range(NB):
                        mm = pe.transpose(dst[0:48, i * P:(i + 1) * P], src[:, i].rearrange("p s e -> p (s e)"),
                                          identb[:])
                    mm.then_inc(slot.full, 1)

                def project(slot, use, w, src, rows=P):
                    slot.claim(pe, b, use)
                    pe.matmul(slot.tile[0:rows, :], w, src, start=True, stop=True).then_inc(slot.full, 1)

                def token_project(slot, use, src, w, n=P):
                    slot.claim(pe, b, use)
                    for i in range(NB):
                        mm = pe.matmul(slot.tile[:, i * n:(i + 1) * n], src(i), w, start=True, stop=True)
                    mm.then_inc(slot.full, 1)

                def xnT_block(i):
                    return xnT[:, 1 + i * P:1 + (i + 1) * P]

                def layer_head(layer):
                    pe.wait_ge(xn_ready, b * 2 + layer + 1)
                    transpose_blocks(A, f"xnT{layer}", lambda i: xn[:, i, :])
                    A.drawn(pe, b, f"xnT{layer}")
                    rows = (P, 32)[layer]
                    wq_, wk_ = ((wq[:], wk[:]), (wqk4[:, 0, :], wqk4[:, 1, :]))[layer]
                    project(BK, f"q{layer}", wq_, xnT[:, 1:], rows)
                    project(CK, f"k{layer}", wk_, xnT[:, 1:], rows)
                    token_project(A, f"router{layer}", xnT_block, (router0, router1)[layer][:], (E0, E1)[layer])
                    token_project(O, f"v{layer}", xnT_block, (wv, v1w)[layer][:])

                def choice_ranks():
                    pe.wait_ge(choice_ready, b + 1)
                    A.claim(pe, b, "rank")
                    for i in range(NB + 1):
                        dst = A.tile[:, i * 32:(i + 1) * 32]
                        if i < NB:
                            pe.matmul(dst, earlier[:], firstb[:, i].rearrange("p k e -> p (k e)"),
                                      start=True, stop=(i == 0))
                        for before in range(i):
                            mm = pe.matmul(dst, onesb[:], firstb[:, before].rearrange("p k e -> p (k e)"),
                                           start=(i == NB and before == 0), stop=(before == i - 1))
                    mm.then_inc(A.full, 1)

                def gated_units(kind, count, up_gate, src, down, sum_use, used_before, layer=None):
                    base = {"moe0": 0, "ffn": E0, "moe1": E0 + NF}[kind]

                    def down_product(e):
                        if layer is None:
                            pair_of((kind, e)).drawn(pe, b, (kind, e))
                        else:
                            (A, BK)[e % 2].drawn(pe, b, (f"w{layer}", e))
                        if e == 0:
                            CK.claim(pe, b, sum_use)
                        hidden = (hid if layer is None else hidw)[:, (base + e) % 2, :]
                        last = e == count - 1
                        pe.matmul(CK.tile[:], down(e), hidden, start=(e == 0), stop=last)\
                            .then_inc(CK.full if last else hid_used, 1)

                    for e in range(count):
                        pair = pair_of((kind, e))
                        pair.claim(pe, b, (kind, e))
                        g, u = up_gate(e)
                        pe.matmul(pair.tile[:, 0, :], g, src, start=True, stop=True)
                        pe.matmul(pair.tile[:, 1, :], u, src, start=True, stop=True).then_inc(pair.full, 1)
                        if layer is not None:
                            if e == 0:
                                if layer == 1:
                                    choice_ranks()
                                pe.wait_ge(w_parts_ready, b * 2 + layer + 1)
                                parts_to_rows(A, f"weightT{layer}", w_parts)
                                A.drawn(pe, b, f"weightT{layer}")
                            project((A, BK)[e % 2], (f"w{layer}", e), pick[:, e, :], weightT[:])
                        if e >= 1:
                            down_product(e - 1)
                    down_product(count - 1)

                def max_pass(layer, heads, D):
                    J = heads // 2
                    pe.wait_ge(stacks_loaded, b * 384 + layer * 192 + 192)
                    for n, (i, h0, count) in enumerate(max_units(heads)):
                        pair = pair_of((f"max{layer}", n))
                        pair.claim(pe, b, (f"max{layer}", n))
                        keys = (i + 1) * P
                        room = 1024 // count
                        flat = pair.tile[:].rearrange("p a t -> p (a t)")
                        for c in range(count):
                            p0, j = 64 * ((h0 + c) // J), (h0 + c) % J
                            q = QS[layer][p0:p0 + COPIES * D, j, i * P:(i + 1) * P]
                            k = KS[layer][p0:p0 + COPIES * D, j, 0:keys]
                            pe.matmul(flat[:, c * room:c * room + keys], q, k, start=True, stop=False)
                            mm = pe.matmul(flat[:, c * room + i * P:c * room + keys], identb[:], future_key[:],
                                           start=False, stop=True)
                        mm.then_inc(pair.full, 1)

                def scores(layer, g, D, J):
                    def piece(dst, h, kb):
                        p0, j = 64 * (h // J), h % J
                        rows = COPIES * D + PARTS
                        pe.matmul(dst, KS[layer][p0:p0 + rows, j, kb * P:(kb + 1) * P],
                                  QS[layer][p0:p0 + rows, j, kb * P:T], start=True, stop=False)
                        return pe.matmul(dst[:, 0:P], identb[:], past_query[:], start=False, stop=True)

                    if g == 0:
                        pe.wait_ge(max_loaded, b * 64 + layer * 32 + 32)
                    for u in range(5):
                        pair = pair_of((f"exp{layer}", g, u))
                        pair.claim(pe, b, (f"exp{layer}", g, u))
                        if u < 4:
                            piece(pair.tile[:, 0, :], 4 * g + u, 0)
                            piece(pair.tile[:, 1, 0:384], 4 * g + u, 1)
                            mm = piece(pair.tile[:, 1, 384:512], 4 * g + u, 3)
                        else:
                            for c in range(4):
                                mm = piece(pair.tile[:, c // 2, 256 * (c % 2):256 * (c % 2) + 256], 4 * g + c, 2)
                        mm.then_inc(pair.full, 1)

                def values(layer, g):
                    pair_of((f"exp{layer}", g, 4)).drawn(pe, b, (f"exp{layer}", g, 4))
                    O.claim(pe, b, (f"pv{layer}", g))
                    pb = probs[:, g % 2]
                    for kb in (0, 1, 3, 2):
                        for c in range(4):
                            src = {0: pb[:, c, 0:512], 1: pb[:, c, 512:896], 3: pb[:, c, 896:1024],
                                   2: pb[:, 4, 256 * c:256 * c + 256]}[kb]
                            mm = pe.matmul(O.tile[32 * c:32 * c + 32, kb * P:T], V[layer][:, kb, 4 * g + c, :], src,
                                           start=(kb == 0), stop=(kb == 2), skip_group_check=True)
                    mm.then_inc(O.full, 1)

                def values_to_tokens(layer, g):
                    O.drawn(pe, b, (f"pv{layer}", g))
                    transpose_blocks(A, (f"attnN{layer}", g), lambda i: attnU[:, g % 2, i * P:(i + 1) * P])

                def attention(layer, groups, D, J):
                    for g in range(groups + 2):
                        if g < groups:
                            scores(layer, g, D, J)
                        if 1 <= g <= groups:
                            values(layer, g - 1)
                        if g >= 2:
                            values_to_tokens(layer, g - 2)
                    pe.wait_ge(attn_ready, b * 2 + layer + 1)
                    transpose_blocks(BK, f"attnT{layer}", lambda i: attn[:, i, :])
                    BK.drawn(pe, b, f"attnT{layer}")

                layer_head(0)
                gated_units("moe0", E0, lambda e: (ew1[:, e, :], ew3[:, e, :]), xnT[:, 1:],
                            lambda e: ew2[:, e, :], "moe0_sum", 0, layer=0)
                max_pass(0, H0, D0)
                CK.drawn(pe, b, "moe0_sum")
                transpose_blocks(BK, "moe0_tok", lambda i: yT[:, i * P:(i + 1) * P])
                pe.wait_ge(max_parts_ready, b * 2 + 1)
                parts_to_rows(A, "maxT0", max_parts)
                pe.wait_ge(mix_ready, b * 3 + 3)
                pair = pair_of("rwkv_kv")
                pair.claim(pe, b, "rwkv_kv")
                pe.matmul(pair.tile[:, 0, :], rk[:], mix[:, 0, :], start=True, stop=True)
                pe.matmul(pair.tile[:, 1, :], rv[:], mix[:, 1, :], start=True, stop=True).then_inc(pair.full, 1)
                pair = pair_of("rwkv_r")
                pair.claim(pe, b, "rwkv_r")
                pe.matmul(pair.tile[:, 0, :], rr[:], mix[:, 2, :], start=True, stop=True).then_inc(pair.full, 1)
                attention(0, G0, D0, J0)
                token_project(A, "o_proj0", lambda i: attnT[:, i * P:(i + 1) * P], wo[:])
                pe.wait_ge(h_ready, b + 1)
                transpose_blocks(BK, "hT", lambda i: hres[:, i, :])
                BK.drawn(pe, b, "hT")
                gated_units("ffn", NF, lambda f: (w1[:, f * P:(f + 1) * P], w3[:, f * P:(f + 1) * P]), hT,
                            lambda f: w2[:, f, :], "ffn_sum", E0 - 1)
                CK.drawn(pe, b, "ffn_sum")
                transpose_blocks(A, "ffn_tok", lambda i: yT[:, i * P:(i + 1) * P])
                pe.wait_ge(rwkv_ready, b + 1)
                token_project(A, "s0", lambda i: rwkvT[:, i * P:(i + 1) * P], ro[:])

                layer_head(1)
                gated_units("moe1", E1, lambda e: (gw[:, e, :], uw[:, e, :]), xnT[:, 1:],
                            lambda e: dw[:, e, :], "moe1_sum", E0 + NF - 2, layer=1)
                max_pass(1, H1, D1)
                CK.drawn(pe, b, "moe1_sum")
                transpose_blocks(BK, "moe1_tok", lambda i: yT[:, i * P:(i + 1) * P])
                pe.wait_ge(max_parts_ready, b * 2 + 2)
                parts_to_rows(A, "maxT1", max_parts)
                attention(1, G1, D1, J1)
                token_project(A, "s1", lambda i: attnT[:, i * P:(i + 1) * P], o1w[:])

        @block.scalar
        def _(act):
            act.wait_ge(weights_loaded, 16 * len(loads))
            act.activation(decay[:], cols[:, 0:1], ACT.Exp).then_inc(decay_exp, 1)
            act.wait_ge(setup_done, 1)

            with act.Fori(0, B) as b:
                def draw(slot, use, dst, src=None, scale=1.0):
                    slot.filled(act, b, use)
                    act.activation(dst, slot.tile[:] if src is None else src, ACT.Copy, scale=scale)\
                        .then_inc(slot.taken, 1)

                def layer_head(layer):
                    draw(A, f"xnT{layer}", xnT[:, 1:])
                    rows = (P, 32)[layer]
                    draw(BK, f"q{layer}", compact[0:rows, 0, :], BK.tile[0:rows, :],
                         scale=(float(D0) ** -0.5, q_scale1[:])[layer])
                    draw(CK, f"k{layer}", compact[0:rows, 1, :], CK.tile[0:rows, :])
                    H = (H0, H1)[layer]
                    draw(O, f"v{layer}", V[layer][:, :, :, 0:P // H],
                         O.tile[:].rearrange("p (i h d) -> p i h d", i=NB, h=H))
                    E = (E0, E1)[layer]
                    act.wait_ge(logits_shifted, b * 2 + layer + 1)
                    act.activation(expl[:, :, 0:E], expl[:, :, 0:E], ACT.Exp).then_inc(expl_ready, 1)
                    draw(A, f"weightT{layer}", weightT[:], A.tile[:].bitcast(BF16)[0:48, 0:T])

                def silus(kind, count):
                    base = {"moe0": 0, "ffn": E0, "moe1": E0 + NF}[kind]
                    for e in range(count):
                        pair = pair_of((kind, e))
                        pair.filled(act, b, (kind, e))
                        if e >= 2:
                            pair_of((kind, e - 2)).drawn(act, b, (kind, e - 2))
                        act.activation(silu[:, (base + e) % 2, :], pair.tile[:, 0, :], ACT.Silu).then_inc(silu_ready, 1)

                def sum_squares(slot, use, n):
                    slot.filled(act, b, use)
                    for i in range(NB):
                        last = act.activation(sq[:, i, :], slot.tile[:, i * P:(i + 1) * P], ACT.Square,
                                              accum_out=ssum[:, n, i:i + 1])
                    last.then_inc(sumsq_ready, 1)

                def exponentials(layer, g):
                    if g >= 2:
                        O.filled(act, b, (f"pv{layer}", g - 2))
                    for u in range(5):
                        pair = pair_of((f"exp{layer}", g, u))
                        pair.filled(act, b, (f"exp{layer}", g, u))
                        act.activation(probs[:, g % 2, u, :], pair.tile[:].rearrange("p a t -> p (a t)"), ACT.Exp)\
                            .then_inc(pair.taken, 1)

                layer_head(0)
                silus("moe0", E0)
                draw(CK, "moe0_sum", yT[:])
                sum_squares(BK, "moe0_tok", 0)
                draw(A, "maxT0", maxT[:], A.tile[:].bitcast(BF16)[0:48, 0:T])
                pair = pair_of("rwkv_kv")
                draw(pair, "rwkv_kv", kv[:])
                pair = pair_of("rwkv_r")
                pair.filled(act, b, "rwkv_r")
                act.activation(er[:], pair.tile[:, 0, :], ACT.Exp, scale=-1.0).then_inc(pair.taken, 1)
                for g in range(G0):
                    exponentials(0, g)
                    if g == 0:
                        for n in range(2):
                            act.wait_ge(expo_args, b * 2 + n + 1)
                            act.activation(expo[:, 2 * n:2 * n + 2, :], expo[:, 2 * n:2 * n + 2, :], ACT.Exp)\
                                .then_inc(expo_ready, 1)
                    if g >= 1:
                        draw(O, ("pv0", g - 1), attnU[:, (g - 1) % 2, :])
                draw(O, ("pv0", G0 - 1), attnU[:, (G0 - 1) % 2, :])
                draw(BK, "attnT0", attnT[:])
                sum_squares(A, "o_proj0", 1)
                draw(BK, "hT", hT)
                silus("ffn", NF)
                draw(CK, "ffn_sum", yT[:])
                sum_squares(A, "ffn_tok", 2)
                act.wait_ge(pre_ready, b + 1)
                act.activation(gate[:], pre, ACT.Silu).then_inc(gate_ready, 1)

                layer_head(1)
                silus("moe1", E1)
                draw(CK, "moe1_sum", yT[:])
                BK.filled(act, b, "moe1_tok")
                act.activation(gate[:].rearrange("p i c -> p (i c)"), BK.tile[:], ACT.Silu).then_inc(BK.taken, 1)
                draw(A, "maxT1", maxT[:], A.tile[:].bitcast(BF16)[0:48, 0:T])
                for g in range(G1):
                    exponentials(1, g)
                    if g >= 1:
                        draw(O, ("pv1", g - 1), attnU[:, (g - 1) % 2, :])
                draw(O, ("pv1", G1 - 1), attnU[:, (G1 - 1) % 2, :])
                draw(BK, "attnT1", attnT[:])
                act.wait_ge(out_ready, b + 1)
                act.dma_start(out_rows[b], x_out[:]).then_inc(out_stored, 16)
            act.wait_ge(out_stored, 16 * B + 16)

        @block.gpsimd
        def _(pool):
            pool.wait_ge(weights_loaded, 16 * len(loads))
            pool.wait_ge(setup_done, 1)
            with pool.Fori(0, B) as b:
                steps = [0]

                def link(ins):
                    steps[0] += 1
                    ins.then_inc(pool_step, 1)
                    pool.wait_ge(pool_step, b * POOL_STEPS + steps[0])

                def inverse_root(dst, src, factor):
                    stand(pool)
                    link(pool.tensor_scalar(ssum_e[:], src, factor, EPS, ALU.mult, ALU.add))
                    return pool.tensor_tensor(dst, ssum_e[:], minus_half[:], ALU.pow)

                def rstd_of_norm(layer):
                    pool.wait_ge(var_ready, b * 2 + layer + 1)
                    inverse_root(rstd[:], meanvar[:, :, 1], 1.0).then_inc(rstd_ready, 1)

                def rms_of(n):
                    pool.wait_ge(sumsq_ready, b * 3 + n + 1)
                    inverse_root(rms[:, n, :], ssum[:, n, :], 1.0 / C).then_inc(rms_ready, 1)

                rstd_of_norm(0)
                A.drawn(pool, b, "xnT0")
                for n in range(3):
                    stand(pool)
                    pool.tensor_scalar(mix_a, xnT[:, 0:T], omix[:, n:n + 1], 0.0, ALU.mult, ALU.add)
                    link(pool.tensor_scalar(mix_b, xnT[:, 1:], cols[:, 2 + n:3 + n], 0.0, ALU.mult, ALU.add))
                    pool.tensor_tensor(mix[:, n, :], mix_b, mix_a, ALU.add).then_inc(mix_ready, 1)
                    pool.wait_ge(mix_ready, b * 3 + n + 1)
                for n in range(3):
                    rms_of(n)
                rstd_of_norm(1)
                assert steps[0] == POOL_STEPS, f"POOL_STEPS {steps[0]}"

        @block.vector
        def _(dve):
            for slot in (*pairs, A, BK, CK, O):
                dve.sem_inc(slot.taken, 1)
            dve.sem_inc(x_in_free, 1)
            dve.sem_inc(out_stored, 16)
            for stack in KS:
                dve.memset(stack[:], 1.0)
            for v, H in zip(V, (H0, H1)):
                dve.memset(v[:], 0.0).then_inc(v_cleared, 1)
            dve.wait_ge(v_cleared, 2)
            for v, H in zip(V, (H0, H1)):
                dve.memset(v[:, :, :, P // H:P // H + 1], 1.0)
            dve.memset(minus_half[:], -0.5)
            dve.memset(taken[:], 0.0)
            dve.memset(w_parts[:], 0.0)
            dve.memset(xnT[:, 0:1], 0.0)
            dve.memset(o_all[:, 0:1], NEG)
            dve.memset(p_all[:, 0:1], 0.0)
            dve.memset(q_all[:, 0:1], 0.0)
            dve.wait_ge(weights_loaded, 16 * len(loads))
            dve.memset(onesb[:], 1.0)
            dve.tensor_copy(identb[:], ident[:])
            for dst, wide in narrow:
                dve.tensor_copy(dst, wide)
            dve.tensor_scalar(omix[:], cols[:, 2:5], -1.0, 1.0, ALU.mult, ALU.add)
            dve.scalar_tensor_tensor(out=q_scale1[:], in0=scale_dims[:, 0:1], scalar=scale[:], in1=scale_dims[:, 1:2],
                                     op0=ALU.mult, op1=ALU.add)
            dve.wait_ge(direction_product, 1)
            dve.tensor_copy(wqk4[:].rearrange("p t d -> p (t d)"), BK.tile[:, 0:64])
            dve.wait_ge(decay_exp, 1)
            dve.tensor_scalar(decay[:], decay[:], -1.0, None, ALU.mult).then_inc(setup_done, 1)
            dve.wait_ge(setup_done, 1)

            with dve.Fori(0, B) as b:
                steps = [0]

                def link(ins):
                    steps[0] += 1
                    ins.then_inc(dve_step, 1)
                    dve.wait_ge(dve_step, b * DVE_STEPS + steps[0])

                def layer_norm(layer, x):
                    for i in range(NB):
                        last = dve.bn_stats(stats[:, i, :], x[:, i, :])
                    link(last)
                    stand(dve)
                    for i in range(NB):
                        last = dve.bn_aggr(meanvar[:, i, :], stats[:, i, :])
                    last.then_inc(var_ready, 1)
                    dve.wait_ge(var_ready, b * 2 + layer + 1)
                    dve.wait_ge(rstd_ready, b * 2 + layer + 1)
                    for i in range(NB):
                        last = dve.tensor_scalar(xn[:, i, :], x[:, i, :], meanvar[:, i, 0:1], rstd[:, i:i + 1],
                                                 ALU.subtract, ALU.mult)
                    last.then_inc(xn_ready, 1)

                def split(dst, value, rest, sign=1.0):
                    link(dve.tensor_scalar(dst(0), value, sign, None, ALU.mult))
                    link(dve.scalar_tensor_tensor(out=rest, in0=value, scalar=sign, in1=dst(0),
                                                  op0=ALU.mult, op1=ALU.subtract))
                    link(dve.tensor_copy(dst(1), rest))
                    link(dve.tensor_tensor(rest, rest, dst(1), ALU.subtract))
                    return dve.tensor_copy(dst(2), rest)

                def split_queries(layer):
                    rows = (P, 32)[layer]
                    CK.drawn(dve, b, f"k{layer}")
                    split(lambda s: parts[0:rows, :, s, :], compact[0:rows], split_rest[0:rows])\
                        .then_inc(parts_ready, 1)

                def router(layer):
                    E = (E0, E1)[layer]

                    def wide(col):
                        return top[:, :, col:col + 1].to_broadcast([P, NB, E])

                    lg, pr, ex = logits[:, :, 0:E], pri[:, :, 0:E], expl[:, :, 0:E]
                    A.filled(dve, b, f"router{layer}")
                    dve.tensor_copy(lg, A.tile[:, 0:NB * E].rearrange("p (i e) -> p i e", e=E)).then_inc(A.taken, 1)
                    A.drawn(dve, b, f"router{layer}")
                    for k in range(2):
                        link(dve.tensor_reduce(top[:, :, 0:1], lg, AX.X, ALU.max))
                        if k == 0:
                            dve.tensor_tensor(ex, lg, wide(0), ALU.subtract).then_inc(logits_shifted, 1)
                        link(dve.tensor_tensor(pr, lg, wide(0), ALU.is_equal))
                        link(dve.tensor_tensor(pr, pr, ramp[:, :, 0:E], ALU.mult))
                        link(dve.tensor_reduce(top[:, :, 1:2], pr, AX.X, ALU.max))
                        link(dve.tensor_tensor(first[:, :, k, 0:E], pr, wide(1), ALU.is_equal))
                        if k == 0:
                            link(dve.scalar_tensor_tensor(out=lg, in0=first[:, :, 0, 0:E], scalar=NEG, in1=lg,
                                                          op0=ALU.mult, op1=ALU.add))
                    dve.wait_ge(expl_ready, b * 2 + layer + 1)
                    link(dve.tensor_reduce(top[:, :, 2:3], ex, AX.X, ALU.add))
                    link(dve.reciprocal(top[:, :, 3:4], top[:, :, 2:3]))
                    link(dve.tensor_tensor(ex, ex, wide(3), ALU.mult))
                    if layer == 1:
                        dve.tensor_copy(firstb[:], first[:]).then_inc(choice_ready, 1)
                        A.filled(dve, b, "rank")
                        taken_row = taken[:].rearrange("p (o k) e -> p o (k e)", o=1)
                        link(dve.tensor_tensor(rank[:].rearrange("p i k e -> p i (k e)"),
                                               A.tile[:, 0:NB * 32].rearrange("p (i n) -> p i n", i=NB),
                                               taken_row.to_broadcast([P, NB, 32]), ALU.add))
                        dve.tensor_tensor(taken[:].rearrange("p k e -> p (k e)"), A.tile[:, NB * 32:(NB + 1) * 32],
                                          taken[:].rearrange("p k e -> p (k e)"), ALU.add).then_inc(A.taken, 1)
                        link(dve.scalar_tensor_tensor(out=first[:].rearrange("p i k e -> p (i k e)"),
                                                      in0=rank[:].rearrange("p i k e -> p (i k e)"), scalar=CAPACITY,
                                                      in1=first[:].rearrange("p i k e -> p (i k e)"),
                                                      op0=ALU.is_lt, op1=ALU.mult))
                    link(dve.tensor_tensor(pr, first[:, :, 0, 0:E], first[:, :, 1, 0:E], ALU.add))
                    link(dve.tensor_tensor(wtop[:, :, 0:E], pr, ex, ALU.mult))
                    split(lambda s: w_parts[:, :, s, 0:E], wtop[:, :, 0:E], w_rest[:, :, 0:E])\
                        .then_inc(w_parts_ready, 1)

                def gated_units(kind, count, used_before, layer=None):
                    base = {"moe0": 0, "ffn": E0, "moe1": E0 + NF}[kind]
                    for e in range(count):
                        pair, n = pair_of((kind, e)), base + e
                        if e >= 2:
                            dve.wait_ge(hid_used, b * HID_WAITS + used_before + e - 1)
                        dve.wait_ge(silu_ready, b * UNITS + n + 1)
                        dve.tensor_tensor(hid[:, n % 2, :], silu[:, n % 2, :], pair.tile[:, 1, :], ALU.mult)\
                            .then_inc(pair.taken, 1)
                        if layer is not None:
                            slot = (A, BK)[e % 2]
                            pair.drawn(dve, b, (kind, e))
                            slot.filled(dve, b, (f"w{layer}", e))
                            dve.tensor_tensor(hidw[:, n % 2, :], hid[:, n % 2, :], slot.tile[:], ALU.mult)\
                                .then_inc(slot.taken, 1)

                def maxima(layer, heads):
                    units = max_units(heads)
                    for n, (i, h0, count) in enumerate(units):
                        pair = pair_of((f"max{layer}", n))
                        pair.filled(dve, b, (f"max{layer}", n))
                        src = pair.tile[:].rearrange("p a t -> p (a t)").rearrange("p (c k) -> p c k", c=count)
                        dve.tensor_reduce(row_max[:, i, h0:h0 + count], src[:, :, 0:(i + 1) * P], AX.X, ALU.max)\
                            .then_inc(pair.taken, 1)
                    for n in (len(units) - 2, len(units) - 1):
                        pair_of((f"max{layer}", n)).drawn(dve, b, (f"max{layer}", n))
                    split(lambda s: max_parts[:, :, s, 0:heads], row_max[:, :, 0:heads], max_rest[:, :, 0:heads], -1.0)\
                        .then_inc(max_parts_ready, 1)

                def rms_scaled(dst, slot, use, n, norm):
                    slot.filled(dve, b, use)
                    dve.wait_ge(rms_ready, b * 3 + n + 1)
                    for i in range(NB):
                        last = dve.scalar_tensor_tensor(out=dst[:, i, :], in0=slot.tile[:, i * P:(i + 1) * P],
                                                        scalar=rms[:, n, i:i + 1], in1=norms[:, norm, :],
                                                        op0=ALU.mult, op1=ALU.mult)
                    last.then_inc(slot.taken, 1)
                    slot.drawn(dve, b, use)

                def normalise_attention(layer, g, groups):
                    d = P // (H0, H1)[layer]
                    A.filled(dve, b, (f"attnN{layer}", g))
                    src = A.tile[:].rearrange("p (i c d) -> p i c d", i=NB, c=4)
                    link(dve.reciprocal(rsum[:], src[:, :, :, d]))
                    dst = attn[:, :, 4 * g * d:4 * (g + 1) * d].rearrange("p i (c d) -> p i c d", c=4)
                    dve.tensor_tensor(dst, src[:, :, :, 0:d], rsum[:].unsqueeze(3).to_broadcast([P, NB, 4, d]), ALU.mult)\
                        .then_inc(A.taken, 1)
                    if g == groups - 1:
                        A.drawn(dve, b, (f"attnN{layer}", g))
                        dve.sem_inc(attn_ready, 1)

                def time_mix_states():
                    k, u, w = kv[:, 0, :], cols[:, 1:2], decay[:]
                    o_before, o_now = o_all[:, 0:T], o_all[:, 1:]
                    pair_of("rwkv_kv").drawn(dve, b, "rwkv_kv")
                    link(dve.tensor_tensor_scan(o_now, w.to_broadcast([P, T]), k, NEG, ALU.add, ALU.max))
                    dve.scalar_tensor_tensor(out=expo[:, 0, :], in0=o_before, scalar=w, in1=o_now,
                                             op0=ALU.add, op1=ALU.subtract)
                    dve.tensor_tensor(expo[:, 1, :], k, o_now, ALU.subtract).then_inc(expo_args, 1)
                    link(dve.scalar_tensor_tensor(out=t1[:], in0=k, scalar=u, in1=o_before, op0=ALU.add, op1=ALU.max))
                    dve.tensor_tensor(expo[:, 2, :], o_before, t1[:], ALU.subtract)
                    dve.scalar_tensor_tensor(out=expo[:, 3, :], in0=k, scalar=u, in1=t1[:],
                                             op0=ALU.add, op1=ALU.subtract).then_inc(expo_args, 1)

                def time_mix_result():
                    v = kv[:, 1, :]
                    dve.wait_ge(expo_ready, b * 2 + 1)
                    link(dve.tensor_tensor(bv[:], expo[:, 1, :], v, ALU.mult))
                    dve.tensor_tensor_scan(q_all[:, 1:], expo[:, 0, :], expo[:, 1, :], 0.0, ALU.mult, ALU.add)
                    link(dve.tensor_tensor_scan(p_all[:, 1:], expo[:, 0, :], bv[:], 0.0, ALU.mult, ALU.add))
                    dve.wait_ge(expo_ready, b * 2 + 2)
                    dve.tensor_tensor(t2[:], expo[:, 2, :], p_all[:, 0:T], ALU.mult)
                    dve.tensor_tensor(t1[:], expo[:, 3, :], v, ALU.mult)
                    link(dve.tensor_tensor(t3[:], expo[:, 2, :], q_all[:, 0:T], ALU.mult))
                    link(dve.tensor_tensor(t3[:], t3[:], expo[:, 3, :], ALU.add))
                    link(dve.tensor_tensor(t1[:], t1[:], t2[:], ALU.add))
                    pair_of("rwkv_r").drawn(dve, b, "rwkv_r")
                    link(dve.scalar_tensor_tensor(out=t3[:], in0=er[:], scalar=1.0, in1=t3[:], op0=ALU.add, op1=ALU.mult))
                    link(dve.reciprocal(t2[:], t3[:]))
                    dve.tensor_tensor(rwkvT[:], t1[:], t2[:], ALU.mult).then_inc(rwkv_ready, 1)

                dve.wait_ge(x_loaded, b * 16 + 16)
                layer_norm(0, x_in)
                split_queries(0)
                router(0)
                gated_units("moe0", E0, 0, layer=0)
                maxima(0, H0)
                rms_scaled(sparse, BK, "moe0_tok", 0, 2)
                time_mix_states()
                normalise_attention(0, 0, G0)
                time_mix_result()
                for g in range(1, G0):
                    normalise_attention(0, g, G0)
                rms_scaled(tok_a, A, "o_proj0", 1, 0)
                link(dve.tensor_tensor(hres, tok_a, xn[:], ALU.add))
                dve.sem_inc(h_ready, 1)
                link(dve.tensor_tensor(pre, hres, sparse[:], ALU.add))
                gated_units("ffn", NF, E0 - 1)
                rms_scaled(tok_a, A, "ffn_tok", 2, 1)
                dve.tensor_tensor(pre, pre, tok_a, ALU.add).then_inc(pre_ready, 1)
                dve.wait_ge(gate_ready, b + 1)
                A.filled(dve, b, "s0")
                dve.tensor_tensor(x_cur[:].rearrange("p i c -> p (i c)"), A.tile[:], gate[:].rearrange("p i c -> p (i c)"),
                                  ALU.mult).then_inc(A.taken, 1)
                A.drawn(dve, b, "s0")
                dve.tensor_tensor(x_cur[:], x_cur[:], x_in[:], ALU.add).then_inc(x_in_free, 1)
                dve.wait_ge(x_in_free, b + 2)

                layer_norm(1, x_cur)
                split_queries(1)
                router(1)
                gated_units("moe1", E1, E0 + NF - 2, layer=1)
                maxima(1, H1)
                for g in range(G1):
                    normalise_attention(1, g, G1)
                A.filled(dve, b, "s1")
                BK.drawn(dve, b, "moe1_tok")
                dve.wait_ge(out_stored, b * 16 + 16)
                dve.tensor_tensor(x_out[:].rearrange("p i c -> p (i c)"), A.tile[:], gate[:].rearrange("p i c -> p (i c)"),
                                  ALU.mult).then_inc(A.taken, 1)
                A.drawn(dve, b, "s1")
                dve.tensor_tensor(x_out[:], x_out[:], x_cur[:], ALU.add).then_inc(out_ready, 1)
                assert steps[0] == DVE_STEPS, f"DVE_STEPS {steps[0]}"


def shape_constants():
    import itertools

    n = np.arange(P)
    pick = np.zeros((48, 16, P), np.float32)
    for e in range(16):
        pick[[e, 16 + e, 32 + e], e, :] = 1
    dirs = np.array(list(itertools.product([-1.0, 1.0], repeat=3)), dtype=np.float32)
    dirs = dirs / np.linalg.norm(dirs, axis=1, keepdims=True)
    m4 = np.zeros((24, 2, 4, 4), np.float32)
    for h in range(8):
        for d in range(3):
            m4[3 * h + d, h // 4, d, h % 4] = 1
            m4[3 * h + d, h // 4, 3, h % 4] = dirs[h, d]
    scaled = np.tile((np.arange(4) < 3).astype(np.float32).repeat(4), 2)
    return {
        "ident": np.eye(P, dtype=np.float32),
        "future_key": np.where(n[None, :] > n[:, None], NEG, 0).astype(np.float32),
        "past_query": np.where(n[None, :] < n[:, None], NEG, 0).astype(np.float32),
        "earlier": (n[:, None] < n[None, :]).astype(np.float32),
        "pick": pick.reshape(48, 16 * P),
        "ramp": np.broadcast_to(16 - np.arange(16, dtype=np.float32), (P, 4, 16)).copy(),
        "m4": m4.reshape(24, 32),
        "scale_dims": np.stack([scaled, 1 - scaled], 1),
    }


def kernel(**inputs):
    import concourse.bacc as bacc
    from concourse.bass_utils import run_bass_kernel_spmd

    x = {k: np.asarray(v) for k, v in inputs.items()}
    L0, L1 = "L0_attn_", "L1_attn_"

    def by_dim(w):
        return np.ascontiguousarray(w.reshape(P, 2, 8, 8).transpose(0, 1, 3, 2).reshape(P, P))

    arrays = {
        "x": x[L0 + "x"],
        "wq": by_dim(x["L0_ffn_wq"]), "wk": by_dim(x["L0_ffn_wk"]), "wv": x["L0_ffn_wv"], "wo": x["L0_ffn_wo"],
        "rk": x[L0 + "Wk"].T, "rv": x[L0 + "Wv"].T, "rr": x[L0 + "Wr"].T, "ro": x[L0 + "Wo"].T,
        "w1": x["L0_ffn_w1"], "w3": x["L0_ffn_w3"], "w2": x["L0_ffn_w2"],
        "router0": x["L0_ffn_router_w"], "ew1": x["L0_ffn_ew1"], "ew2": x["L0_ffn_ew2"], "ew3": x["L0_ffn_ew3"],
        "Wq1": x[L1 + "Wq"], "Wk1": x[L1 + "Wk"], "v1w": x[L1 + "Wv"].T, "o1w": x[L1 + "Wo"].T,
        "scale": x[L1 + "scale"].reshape(1, 1),
        "router1": x["L1_ffn_router_w"], "gate_w": x["L1_ffn_gate_w"], "up_w": x["L1_ffn_up_w"],
        "down_w": x["L1_ffn_down_w"],
        **{n: x[L0 + n] for n in ("time_decay", "time_first")},
        **{n: x[L0 + n].reshape(P) for n in ("time_mix_k", "time_mix_v", "time_mix_r")},
        **{n: x["L0_ffn_" + n] for n in ("attn_norm_w", "ff_norm_w", "moe_norm_w")},
        **shape_constants(),
    }
    nc = bacc.Bacc("TRN2", target_bir_lowering=False, num_devices=1)
    arrays = {f"in_{k}": np.ascontiguousarray(v) for k, v in arrays.items()}
    args = {k[3:]: nc.dram_tensor(k, v.shape, mybir.dt.from_np(v.dtype), kind="ExternalInput").ap()
            for k, v in arrays.items()}
    out = nc.dram_tensor("out_0", x[L0 + "x"].shape, F32, kind="ExternalOutput").ap()
    build(nc, args, out)
    r = run_bass_kernel_spmd(nc, [arrays], core_ids=[0])
    return r.results[0]["out_0"]
```

```python
from contextlib import ExitStack

import numpy as np

import concourse.bass as bass
import concourse.mybir as mybir

F32 = mybir.dt.float32
BF16 = mybir.dt.bfloat16
ALU = mybir.AluOpType
ACT = mybir.ActivationFunctionType
AX = mybir.AxisListType

P = 128
EPS = 1e-5
NEG = -1e38

Q_RUNS = [(0, 3, 0, 0), (3, 2, 1, 0), (5, 1, 2, 0)]
K_RUNS = [(0, 3, 0, 1), (3, 2, 0, 1), (5, 1, 0, 0)]
COPIES, PARTS = 6, 3
STACK_DMAS = 12


class Slot:

    def __init__(self, tile, full, taken, uses):
        self.tile, self.full, self.taken, self.uses = tile, full, taken, list(uses)
        self.per_row = len(self.uses)

    def claim(self, pe, row, use):
        pe.wait_ge(self.taken, row * self.per_row + self.uses.index(use) + 1)

    def filled(self, eng, row, use):
        eng.wait_ge(self.full, row * self.per_row + self.uses.index(use) + 1)

    def drawn(self, eng, row, use):
        eng.wait_ge(self.taken, row * self.per_row + self.uses.index(use) + 2)


def max_units(heads):
    out = []
    for i, n in ((3, 1), (2, 1), (1, 2), (0, 4)):
        out += [(i, h, n) for h in range(0, heads, n)]
    return out


PACE = {"norm": 50, "xnT": 14, "qk": 20, "router": 20, "rank": 15, "weights": 15, "unit": 32, "down": 9, "split": 5,
        "stacks": 5, "v": 9, "max": 6, "max_split": 2, "max_rows": 10, "rwkv_proj": 26, "max_load": 5,
        "exp": 6, "values": 30, "turn": 10, "attnT": 15, "oproj": 60, "hT": 15, "ffn": 30, "ffn_down": 9,
        "ffn_tok": 40, "s": 9, "end": 20}


def merged(front, back):
    out, done = [], [0, 0]
    lists = [list(front), list(back)]
    total = [sum(PACE.get(step[0], 2) for step in x) for x in lists]
    while any(lists):
        side = min((n for n in range(2) if lists[n]), key=lambda n: done[n] / total[n])
        step = lists[side].pop(0)
        out.append((("front", "back")[side], step))
        done[side] += PACE.get(step[0], 2)
    return out


def spread(steps, among):
    out, at = [], 0
    for n, x in enumerate(among):
        out.append(x)
        while at < len(steps) and (at + 1) * len(among) <= (n + 1) * len(steps):
            out.append(steps[at])
            at += 1
    return out


def plan_of(layer, heads, experts, ffn_units):
    groups = heads // 4
    downs = [("down", e) for e in range(experts)]

    def units(e0, e1):
        out = []
        for e in range(e0, e1):
            out.append(("unit", e))
            if e:
                out.append(downs[e - 1])
        return out

    half = (4, 7)[layer]
    front_a = [("norm",), ("xnT",), ("router",), ("qk",), ("split",), *units(0, 1)]
    front_a += ([("rank",)] if layer else []) + [("weights",)]
    front_a += ([("mix",)] if layer == 0 else []) + units(1, half)
    front_b = [("stacks",), ("v",), *units(half, half + 2)]
    rest = units(half + 2, experts - 1)
    front_b += spread(rest, [("max", n) for n in range(len(max_units(heads)))]) + [("max_split",)]
    front_b += [("unit", experts - 1), ("down", experts - 2), ("max_rows",)]
    front_b += ([("rwkv_proj",)] if layer == 0 else []) + [("down", experts - 1), ("max_load",), ("experts_tok",)]

    back_a = []
    for g in range(groups + 1):
        if g < groups:
            back_a += [("exp", g, u) for u in range(5)]
        if g >= 2:
            back_a.append(("turn", g - 2))
        if g < groups:
            back_a += [("exp", g, u) for u in range(5, 10)]
        if g == 0 and layer == 0:
            back_a.append(("states",))
        if g >= 1:
            back_a.append(("values", g - 1))
        if g == 1 and layer == 0:
            back_a.append(("time_mix",))
    back_b = [("turn", groups - 1), ("attnT",)]
    if layer == 0:
        back_b += [("oproj",), ("hT",)]
        for f in range(ffn_units):
            back_b.append(("ffn", f))
            if f:
                back_b.append(("ffn_down", f - 1))
        back_b += [("ffn_down", ffn_units - 1), ("ffn_tok",)]
    back_b += [("s",), ("end",)]
    return [("back", ("keep",))] + merged(front_a, back_a) + merged(front_b, back_b)


def step_uses(layer, step):
    name, n = step[0], step[1:]
    return {
        "xnT": ["xnT"], "qk": ["q", "k"], "router": ["router"], "rank": ["rank"], "weights": ["weights", ("weight", 0)],
        "unit": [("gate", *n), ("up", *n)] + ([("weight", *n)] if n and n[0] else []), "v": ["v"], "max": [("max", *n)], "max_rows": ["max_rows"],
        "rwkv_proj": ["rk", "rv", "rr"], "experts_tok": ["experts_tok"],
        "exp": [("exp", *n)], "turn": [("turn", *n)], "attnT": ["attnT"], "oproj": ["oproj"], "hT": ["hT"],
        "ffn": [("gate", *n), ("up", *n)], "ffn_tok": ["ffn_tok"], "s": ["s"],
    }.get(name, [])


def build_layer(nc, a, layer, x_src, x_dst, capacity):
    B, T, C = x_src.shape
    NB = T // P
    H = (16, 8)[layer]
    D = (8, 4)[layer]
    DV = P // H
    J = H // 2
    G = H // 4
    ROWS = H * D
    E = a[("ew1", "gate_w")[layer]].shape[0]
    FF = a["w1"].shape[1]
    NF = FF // P
    plan = plan_of(layer, H, E, NF)

    with ExitStack() as ctx:
        def sb(name, shape, dt=F32):
            return ctx.enter_context(nc.sbuf_tensor(f"{name}_{layer}", shape, dt))

        def sem(name):
            return ctx.enter_context(nc.semaphore(f"{name}_{layer}"))

        ident = sb("ident", [P, P])
        identb = sb("identb", [P, P], BF16)
        future_key = sb("future_key", [P, P], BF16)
        past_query = sb("past_query", [P, P], BF16)
        earlier = sb("earlier", [P, P], BF16)
        onesb = sb("onesb", [P, P], BF16)
        pick = sb("pick", [48, 16, P], BF16)
        ramp = sb("ramp", [P, NB, 16])
        wv = sb("wv", [P, P])
        router = sb("router", [P, E])
        we_gate, we_up, we_down = (sb(n, [P, E, P]) for n in ("we_gate", "we_up", "we_down"))
        minus_half = sb("minus_half", [P, NB])
        if layer == 0:
            wq, wk, wo = (sb(n, [P, P]) for n in ("wq", "wk", "wo"))
            rk, rv, rr, ro = (sb(n, [P, P]) for n in ("rk", "rv", "rr", "ro"))
            w1, w3, w2 = sb("w1", [P, FF]), sb("w3", [P, FF]), sb("w2", [P, NF, P])
            norms = sb("norms", [P, 3, C])
            cols = sb("cols", [P, 5])
            decay = sb("decay", [P, 1])
            omix = sb("omix", [P, 3])
        else:
            m4 = sb("m4", [24, 32])
            wqk3 = sb("wqk3", [24, 2, P])
            wqk4 = sb("wqk4", [P, 2, 32])
            o1w = sb("o1w", [P, P])
            scale = sb("scale", [32, 1])
            scale_dims = sb("scale_dims", [32, 2])
            q_scale1 = sb("q_scale1", [32, 1])

        x_in = sb("x_in", [P, NB, C])
        stats = sb("stats", [P, NB, 6])
        meanvar = sb("meanvar", [P, NB, 2])
        rstd = sb("rstd", [P, NB])
        xn = sb("xn", [P, NB, C])
        xnT = sb("xnT", [P, 1 + T])
        compact = sb("compact", [P, 2, T])
        split_rest = sb("split_rest", [P, 2, T])
        parts = sb("parts", [P, 2, PARTS, T], BF16)
        row_max = sb("row_max", [P, NB, 16])
        max_rest = sb("max_rest", [P, NB, 16])
        max_parts = sb("max_parts", [P, NB, PARTS, 16], BF16)
        maxT = sb("maxT", [48, T], BF16)
        logits = sb("logits", [P, NB, 16])
        pri = sb("pri", [P, NB, 16])
        first = sb("first", [P, NB, 2, 16])
        top = sb("top", [P, NB, 4])
        expl = sb("expl", [P, NB, 16])
        wtop = sb("wtop", [P, NB, 16])
        w_rest = sb("w_rest", [P, NB, 16])
        w_parts = sb("w_parts", [P, NB, PARTS, 16], BF16)
        weightT = sb("weightT", [48, T], BF16)
        firstb = sb("firstb", [P, NB, 2, 16], BF16)
        rank = sb("rank", [P, NB, 2, 16])
        taken = sb("taken", [P, 2, 16])
        tanh_e = sb("tanh_e", [P, 2, T])
        hidden_e = sb("hidden_e", [P, 2, T])
        expertsT = sb("expertsT", [P, T])
        experts = sb("experts", [P, NB, C])
        sq = sb("sq", [P, NB, C])
        ssum = sb("ssum", [P, 3, NB])
        ssum_e = sb("ssum_e", [P, NB])
        rms = sb("rms", [P, 3, NB])
        if layer == 0:
            mix = sb("mix", [P, 3, T])
            mix_a, mix_b = sb("mix_a", [P, T]), sb("mix_b", [P, T])
        else:
            gate_tanh = sb("gate_tanh", [P, T])

        Q = sb("q_stack", [P, J, T], BF16)
        K = sb("k_stack", [P, J, T], BF16)
        V = sb("v", [P, NB, H, 32])
        if layer == 0:
            kv = sb("kv", [P, 2, T])
            er = sb("er", [P, T])

        x_res = sb("x_res", [P, NB, C])
        probs = sb("probs", [P, 2, 10, 512])
        attnU = sb("attnU", [P, 2, T])
        rsum = sb("rsum", [P, NB, 4])
        attn = sb("attn", [P, NB, C])
        attnT = sb("attnT", [P, T])
        x_out = sb("x_out", [P, NB, C])
        if layer == 0:
            xn_kept = sb("xn_kept", [P, NB, C])
            o_all = sb("o_all", [P, 1 + T])
            p_all = sb("p_all", [P, 1 + T])
            q_all = sb("q_all", [P, 1 + T])
            expo = sb("expo", [P, 4, T])
            t1, t2 = sb("t1", [P, T]), sb("t2", [P, T])
            rwkvT = sb("rwkvT", [P, T])
            tok_a = sb("tok_a", [P, NB, C])
            hres = sb("hres", [P, NB, C])
            hT = sb("hT", [P, T])
            pre = sb("pre", [P, NB, C])
            gate = sb("gate", [P, NB, C])
            tanh_f = sb("tanh_f", [P, 2, T])
            ffnT = attnT

        qk_dram = nc.dram_tensor(f"qk_scratch{layer}", [2, PARTS, P, T], BF16, kind="Internal").ap()
        max_dram = nc.dram_tensor(f"max_scratch{layer}", [48, T], BF16, kind="Internal").ap()

        def psum(name):
            return ctx.enter_context(nc.psum_tensor(f"{name}_{layer}", [P, T], F32))

        def ring(stage):
            order = [u for where, step in plan if where == stage for u in step_uses(layer, step)]
            slots = [Slot(psum(f"{stage}{n}"), sem(f"{stage}{n}_full"), sem(f"{stage}{n}_taken"), order[n::3])
                     for n in range(3)]
            return {use: slots[n % 3] for n, use in enumerate(order)}, slots

        front, front_slots = ring("front")
        back, back_slots = ring("back")
        SUM = Slot(psum("experts_sum"), sem("experts_sum_full"), sem("experts_sum_taken"), ["sum"])
        OUT = Slot(psum("values_bank"), sem("values_bank_full"), sem("values_bank_taken"),
                   [("values", g) for g in range(G)] + ([] if layer else ["ffn_sum"]))

        weights_loaded = sem("weights_loaded")
        direction_product = sem("direction_product")
        decay_exp = sem("decay_exp")
        setup_done = sem("setup_done")
        v_cleared = sem("v_cleared")
        x_loaded = sem("x_loaded")
        res_loaded = sem("res_loaded")
        var_ready = sem("var_ready")
        rstd_ready = sem("rstd_ready")
        xn_ready = sem("xn_ready")
        parts_ready = sem("parts_ready")
        parts_stored = sem("parts_stored")
        stacks_loaded = sem("stacks_loaded")
        max_parts_ready = sem("max_parts_ready")
        max_stored = sem("max_stored")
        max_loaded = sem("max_loaded")
        logits_shifted = sem("logits_shifted")
        expl_ready = sem("expl_ready")
        choice_ready = sem("choice_ready")
        w_parts_ready = sem("w_parts_ready")
        tanh_e_ready = sem("tanh_e_ready")
        hidden_e_used = sem("hidden_e_used")
        tanh_f_ready = sem("tanh_f_ready")
        hidden_f_used = sem("hidden_f_used")
        sumsq_experts = sem("sumsq_experts")
        sumsq_back = sem("sumsq_back")
        rms_experts = sem("rms_experts")
        rms_back = sem("rms_back")
        attn_ready = sem("attn_ready")
        h_ready = sem("h_ready")
        mix_ready = sem("mix_ready")
        expo_args = sem("expo_args")
        expo_ready = sem("expo_ready")
        rwkv_ready = sem("rwkv_ready")
        pre_ready = sem("pre_ready")
        gate_ready = sem("gate_ready")
        out_ready = sem("out_ready")
        out_stored = sem("out_stored")
        waits_met = sem("waits_met")
        dve_front_step, dve_back_step = sem("dve_front_step"), sem("dve_back_step")
        pool_front_step, pool_back_step = sem("pool_front_step"), sem("pool_back_step")
        STEPS = ({"dve_front": 29, "dve_back": 16, "pool_front": 5, "pool_back": 2},
                 {"dve_front": 31, "dve_back": 2, "pool_front": 1, "pool_back": 0})[layer]

        def stand(eng):
            eng.sem_inc(waits_met, 1)

        def chain(eng, name, semaphore, row):
            count = [0]

            def link(ins):
                count[0] += 1
                ins.then_inc(semaphore, 1)
                eng.wait_ge(semaphore, row * STEPS[name] + count[0])

            return link, count

        def run(steps_of, rows):
            does = {stage: steps_of(stage, row) for stage, row in rows.items()}
            for stage, step in plan:
                if stage in does and step[0] in does[stage]:
                    does[stage][step[0]](*step[1:])

        def all_rows(eng, steps_of):
            run(steps_of, {"front": 0})
            with eng.Fori(0, B - 1) as i:
                run(steps_of, {"front": i + 1, "back": i})
            run(steps_of, {"back": B - 1})

        loads = []

        def load(dst, src):
            loads.append((dst, src))

        wide_room = probs[:].rearrange("p g u t -> p (g u t)")
        narrow = [(future_key[:], wide_room[:, 0:P]), (past_query[:], wide_room[:, P:2 * P]),
                  (earlier[:], wide_room[:, 2 * P:3 * P]),
                  (pick[:].rearrange("p e n -> p (e n)"), wide_room[0:48, 4 * P:20 * P])]
        for (_, wide), src in zip(narrow, ("future_key", "past_query", "earlier", "pick")):
            load(wide, a[src])
        load(ident[:], a["ident"])
        load(ramp[:], a["ramp"])
        for dst, src in zip((we_gate, we_up, we_down), (("ew1", "ew3", "ew2"), ("gate_w", "up_w", "down_w"))[layer]):
            load(dst[:], a[src].rearrange("e p h -> p e h"))
        if layer == 0:
            for dst, src in ((wq, "wq"), (wk, "wk"), (wv, "wv"), (wo, "wo"), (rk, "rk"), (rv, "rv"), (rr, "rr"),
                             (ro, "ro"), (w1, "w1"), (w3, "w3"), (router, "router0")):
                load(dst[:], a[src])
            load(w2[:], a["w2"].rearrange("(f p) d -> p f d", p=P))
            for n, src in enumerate(("attn_norm_w", "ff_norm_w", "moe_norm_w")):
                load(norms[:, n, :], a[src].rearrange("(o c) -> o c", o=1).to_broadcast([P, C]))
            for n, src in enumerate(("time_decay", "time_first", "time_mix_k", "time_mix_v", "time_mix_r")):
                load(cols[:, n:n + 1], a[src].rearrange("(c o) -> c o", o=1))
        else:
            for dst, src in ((m4, "m4"), (scale_dims, "scale_dims"), (wv, "v1w"), (o1w, "o1w"), (router, "router1")):
                load(dst[:], a[src])
            load(wqk3[:, 0, :], a["Wq1"])
            load(wqk3[:, 1, :], a["Wk1"])
            load(scale[:], a["scale"].to_broadcast([32, 1]))

        x_rows = x_src.rearrange("b (i p) c -> b p i c", p=P)
        out_rows = x_dst.rearrange("b (i p) c -> b p i c", p=P)

        block = ctx.enter_context(nc.Block())

        def later(row, eng, semaphore, value):
            if not isinstance(row, int) or row > 0:
                eng.wait_ge(semaphore, value)

        @block.sync
        def _(sp):
            for dst, src in loads:
                sp.dma_start(dst, src).then_inc(weights_loaded, 16)

            def steps_of(stage, row):
                def norm():
                    later(row, sp, xn_ready, row)
                    sp.dma_start(x_in[:], x_rows[row]).then_inc(x_loaded, 16)

                def stacks():
                    sp.wait_ge(parts_ready, row + 1)
                    for t in range(2):
                        sp.dma_start(qk_dram[t, :, 0:ROWS, :].rearrange("s p t -> p s t"),
                                     parts[0:ROWS, t]).then_inc(parts_stored, 16)
                    sp.wait_ge(parts_stored, row * 32 + 32)
                    last = ("exp", G - 1, 9)
                    later(row, sp, back[last].full, (row - 1) * back[last].per_row + back[last].uses.index(last) + 1)
                    for t, (stack, runs) in enumerate(((Q, Q_RUNS), (K, K_RUNS))):
                        for half in range(2):
                            for c0, n, part, step in runs:
                                src = qk_dram[t, part:part + (n if step else 1), half * D * J:(half + 1) * D * J, :]
                                src = src.rearrange("s (d j) t -> s d (j t)", d=D)
                                if not step and n > 1:
                                    src = src.to_broadcast([n, D, J * T])
                                p0 = 64 * half + c0 * D
                                sp.dma_start(stack[p0:p0 + n * D].rearrange("p j t -> p (j t)"), src)\
                                    .then_inc(stacks_loaded, 16)

                def max_load():
                    front["max_rows"].drawn(sp, row, "max_rows")
                    sp.dma_start(max_dram, maxT[:]).then_inc(max_stored, 16)
                    sp.wait_ge(max_stored, row * 16 + 16)
                    for half in range(2):
                        p0 = 64 * half + COPIES * D
                        src = max_dram.rearrange("(s h) t -> s h t", s=PARTS)[:, half * J:(half + 1) * J, :]
                        sp.dma_start(Q[p0:p0 + PARTS], src).then_inc(max_loaded, 16)

                def keep():
                    later(row, sp, out_ready, row)
                    sp.dma_start(x_res[:], x_rows[row]).then_inc(res_loaded, 16)

                if stage == "front":
                    return {"norm": norm, "stacks": stacks, "max_load": max_load}
                return {"keep": keep}

            all_rows(sp, steps_of)

        @block.tensor
        def _(pe):
            pe.wait_ge(weights_loaded, 16 * len(loads))
            if layer == 1:
                for t in range(2):
                    mm = pe.matmul(front_slots[0].tile[:, 32 * t:32 * t + 32], wqk3[:, t, :], m4[:], start=True, stop=True)
                mm.then_inc(direction_product, 1)
            pe.wait_ge(setup_done, 1)

            def steps_of(stage, row):
                slots = front if stage == "front" else back

                def transpose_blocks(use, src):
                    slot = slots[use]
                    slot.claim(pe, row, use)
                    for i in range(NB):
                        mm = pe.transpose(slot.tile[:, i * P:(i + 1) * P], src(i), ident[:])
                    mm.then_inc(slot.full, 1)

                def parts_to_rows(use, src):
                    slot = slots[use]
                    slot.claim(pe, row, use)
                    stand(pe)
                    dst = slot.tile[:].bitcast(BF16)
                    for i in range(NB):
                        mm = pe.transpose(dst[0:48, i * P:(i + 1) * P], src[:, i].rearrange("p s e -> p (s e)"),
                                          identb[:])
                    mm.then_inc(slot.full, 1)

                def project(use, w, src, rows=P):
                    slot = slots[use]
                    slot.claim(pe, row, use)
                    pe.matmul(slot.tile[0:rows, :], w, src, start=True, stop=True).then_inc(slot.full, 1)

                def token_project(use, src, w, n=P):
                    slot = slots[use]
                    slot.claim(pe, row, use)
                    for i in range(NB):
                        mm = pe.matmul(slot.tile[:, i * n:(i + 1) * n], src(i), w, start=True, stop=True)
                    mm.then_inc(slot.full, 1)

                def xnT_block(i):
                    return xnT[:, 1 + i * P:1 + (i + 1) * P]

                def turn_norm():
                    pe.wait_ge(xn_ready, row + 1)
                    transpose_blocks("xnT", lambda i: xn[:, i, :])

                def expert_logits():
                    front["xnT"].drawn(pe, row, "xnT")
                    token_project("router", xnT_block, router[:], E)

                def queries_keys():
                    rows = (P, 32)[layer]
                    for use, w in zip("qk", ((wq[:], wk[:]) if layer == 0 else (wqk4[:, 0, :], wqk4[:, 1, :]))):
                        project(use, w, xnT[:, 1:], rows)

                def choice_ranks():
                    pe.wait_ge(choice_ready, row + 1)
                    slot = front["rank"]
                    slot.claim(pe, row, "rank")
                    for i in range(NB + 1):
                        dst = slot.tile[:, i * 32:(i + 1) * 32]
                        if i < NB:
                            pe.matmul(dst, earlier[:], firstb[:, i].rearrange("p k e -> p (k e)"),
                                      start=True, stop=(i == 0))
                        for before in range(i):
                            mm = pe.matmul(dst, onesb[:], firstb[:, before].rearrange("p k e -> p (k e)"),
                                           start=(i == NB and before == 0), stop=(before == i - 1))
                    mm.then_inc(slot.full, 1)

                def expert_weights():
                    pe.wait_ge(w_parts_ready, row + 1)
                    parts_to_rows("weights", w_parts)

                def expert_unit(e):
                    project(("gate", e), we_gate[:, e, :], xnT[:, 1:])
                    project(("up", e), we_up[:, e, :], xnT[:, 1:])

                def expert_weight(e):
                    if e == 0:
                        front["weights"].drawn(pe, row, "weights")
                    project(("weight", e), pick[:, e, :], weightT[:])

                def expert_down(e):
                    front[("weight", e)].drawn(pe, row, ("weight", e))
                    if e == 0:
                        SUM.claim(pe, row, "sum")
                    last = e == E - 1
                    pe.matmul(SUM.tile[:], we_down[:, e, :], hidden_e[:, e % 2, :], start=(e == 0), stop=last)\
                        .then_inc(SUM.full if last else hidden_e_used, 1)

                def max_unit(n):
                    if n == 0:
                        pe.wait_ge(stacks_loaded, row * 16 * STACK_DMAS + 16 * STACK_DMAS)
                    i, h0, count = max_units(H)[n]
                    slot = front[("max", n)]
                    slot.claim(pe, row, ("max", n))
                    keys = (i + 1) * P
                    for c in range(count):
                        p0, j, c0 = 64 * ((h0 + c) // J), (h0 + c) % J, c * (T // count)
                        q = Q[p0:p0 + COPIES * D, j, i * P:(i + 1) * P]
                        k = K[p0:p0 + COPIES * D, j, 0:keys]
                        pe.matmul(slot.tile[:, c0:c0 + keys], q, k, start=True, stop=False)
                        mm = pe.matmul(slot.tile[:, c0 + i * P:c0 + keys], identb[:], future_key[:],
                                       start=False, stop=True)
                    mm.then_inc(slot.full, 1)

                def max_rows():
                    pe.wait_ge(max_parts_ready, row + 1)
                    parts_to_rows("max_rows", max_parts)

                def time_mix_projections():
                    for n, (use, w) in enumerate((("rk", rk), ("rv", rv), ("rr", rr))):
                        pe.wait_ge(mix_ready, row * 3 + n + 1)
                        project(use, w[:], mix[:, n, :])

                def experts_tokens():
                    SUM.drawn(pe, row, "sum")
                    transpose_blocks("experts_tok", lambda i: expertsT[:, i * P:(i + 1) * P])

                def scores(g, u):
                    def piece(dst, h, kb):
                        p0, j = 64 * (h // J), h % J
                        rows = COPIES * D + PARTS
                        pe.matmul(dst, K[p0:p0 + rows, j, kb * P:(kb + 1) * P], Q[p0:p0 + rows, j, kb * P:T],
                                  start=True, stop=False)
                        return pe.matmul(dst[:, 0:P], identb[:], past_query[:], start=False, stop=True)

                    if (g, u) == (0, 0):
                        pe.wait_ge(max_loaded, row * 32 + 32)
                    slot = back[("exp", g, u)]
                    slot.claim(pe, row, ("exp", g, u))
                    if u < 8 and u % 2 == 0:
                        mm = piece(slot.tile[:], 4 * g + u // 2, 0)
                    elif u < 8:
                        piece(slot.tile[:, 0:384], 4 * g + u // 2, 1)
                        mm = piece(slot.tile[:, 384:512], 4 * g + u // 2, 3)
                    else:
                        for c in range(2):
                            mm = piece(slot.tile[:, 256 * c:256 * c + 256], 4 * g + 2 * (u - 8) + c, 2)
                    mm.then_inc(slot.full, 1)

                def values(g):
                    back[("exp", g, 9)].drawn(pe, row, ("exp", g, 9))
                    OUT.claim(pe, row, ("values", g))
                    pb = probs[:, g % 2]
                    for kb in (0, 1, 3, 2):
                        for c in range(4):
                            src = {0: pb[:, 2 * c, :], 1: pb[:, 2 * c + 1, 0:384], 3: pb[:, 2 * c + 1, 384:512],
                                   2: pb[:, 8 + c // 2, 256 * (c % 2):256 * (c % 2) + 256]}[kb]
                            mm = pe.matmul(OUT.tile[32 * c:32 * c + 32, kb * P:T], V[:, kb, 4 * g + c, :], src,
                                           start=(kb == 0), stop=(kb == 2), skip_group_check=True)
                    mm.then_inc(OUT.full, 1)

                def turn_values(g):
                    OUT.drawn(pe, row, ("values", g))
                    transpose_blocks(("turn", g), lambda i: attnU[:, g % 2, i * P:(i + 1) * P])

                def turn_attention():
                    pe.wait_ge(attn_ready, row + 1)
                    transpose_blocks("attnT", lambda i: attn[:, i, :])

                def out_projection():
                    back["attnT"].drawn(pe, row, "attnT")
                    token_project("oproj", lambda i: attnT[:, i * P:(i + 1) * P], wo[:])

                def turn_h():
                    pe.wait_ge(h_ready, row + 1)
                    transpose_blocks("hT", lambda i: hres[:, i, :])

                def ffn_unit(f):
                    if f == 0:
                        back["hT"].drawn(pe, row, "hT")
                    project(("gate", f), w1[:, f * P:(f + 1) * P], hT[:])
                    project(("up", f), w3[:, f * P:(f + 1) * P], hT[:])

                def ffn_down(f):
                    back[("up", f)].drawn(pe, row, ("up", f))
                    if f == 0:
                        OUT.claim(pe, row, "ffn_sum")
                    last = f == NF - 1
                    pe.matmul(OUT.tile[:], w2[:, f, :], tanh_f[:, f % 2, :], start=(f == 0), stop=last)\
                        .then_inc(OUT.full if last else hidden_f_used, 1)

                def ffn_tokens():
                    OUT.drawn(pe, row, "ffn_sum")
                    transpose_blocks("ffn_tok", lambda i: ffnT[:, i * P:(i + 1) * P])

                def branch_output():
                    if layer == 0:
                        pe.wait_ge(rwkv_ready, row + 1)
                        token_project("s", lambda i: rwkvT[:, i * P:(i + 1) * P], ro[:])
                    else:
                        back["attnT"].drawn(pe, row, "attnT")
                        token_project("s", lambda i: attnT[:, i * P:(i + 1) * P], o1w[:])

                if stage == "front":
                    def unit(e):
                        expert_unit(e)
                        if e:
                            expert_weight(e)

                    def weights():
                        expert_weights()
                        expert_weight(0)

                    return {"xnT": turn_norm, "qk": queries_keys,
                            "router": expert_logits,
                            "rank": choice_ranks, "weights": weights, "unit": unit, "down": expert_down,
                            "v": lambda: token_project("v", xnT_block, wv[:]), "max": max_unit, "max_rows": max_rows,
                            "rwkv_proj": time_mix_projections, "experts_tok": experts_tokens}
                return {"exp": scores, "values": values, "turn": turn_values, "attnT": turn_attention,
                        "oproj": out_projection, "hT": turn_h, "ffn": ffn_unit, "ffn_down": ffn_down,
                        "ffn_tok": ffn_tokens, "s": branch_output}

            all_rows(pe, steps_of)

        @block.scalar
        def _(act):
            act.wait_ge(weights_loaded, 16 * len(loads))
            if layer == 0:
                act.activation(decay[:], cols[:, 0:1], ACT.Exp).then_inc(decay_exp, 1)
            act.wait_ge(setup_done, 1)

            def steps_of(stage, row):
                slots = front if stage == "front" else back

                def draw(use, dst, src=None, scale=1.0, slot=None):
                    slot = slot or slots[use]
                    slot.filled(act, row, use)
                    act.activation(dst, slot.tile[:] if src is None else src, ACT.Copy, scale=scale)\
                        .then_inc(slot.taken, 1)

                def queries_keys():
                    rows = (P, 32)[layer]
                    draw("q", compact[0:rows, 0, :], front["q"].tile[0:rows, :],
                         scale=(float(D) ** -0.5 if layer == 0 else q_scale1[:]))
                    draw("k", compact[0:rows, 1, :], front["k"].tile[0:rows, :])

                def router_exp():
                    act.wait_ge(logits_shifted, row + 1)
                    act.activation(expl[:, :, 0:E], expl[:, :, 0:E], ACT.Exp).then_inc(expl_ready, 1)

                def weights():
                    draw("weights", weightT[:], front["weights"].tile[:].bitcast(BF16)[0:48, 0:T])

                def tanh_unit(e):
                    slot = slots[("gate", e)]
                    slot.filled(act, row, ("gate", e))
                    if e >= 2:
                        slots[("weight", e - 2)].drawn(act, row, ("weight", e - 2))
                    act.activation(tanh_e[:, e % 2, :], slot.tile[:], ACT.Tanh, scale=0.5).then_inc(tanh_e_ready, 1)

                def tanh_ffn(f):
                    slot = slots[("gate", f)]
                    slot.filled(act, row, ("gate", f))
                    if f >= 2:
                        act.wait_ge(hidden_f_used, row * (NF - 1) + f - 1)
                    act.activation(tanh_f[:, f % 2, :], slot.tile[:], ACT.Tanh, scale=0.5).then_inc(tanh_f_ready, 1)

                def draw_values():
                    last = ("values", G - 1)
                    later(row, act, OUT.full, (row - 1) * OUT.per_row + OUT.uses.index(last) + 1)
                    draw("v", V[:, :, :, 0:DV], front["v"].tile[:].rearrange("p (i h d) -> p i h d", i=NB, h=H))

                def max_rows():
                    draw("max_rows", maxT[:], front["max_rows"].tile[:].bitcast(BF16)[0:48, 0:T])

                def time_mix_draw():
                    later(row, act, rwkv_ready, row)
                    draw("rk", kv[:, 0, :])
                    draw("rv", kv[:, 1, :])
                    slot = front["rr"]
                    slot.filled(act, row, "rr")
                    act.activation(er[:], slot.tile[:], ACT.Exp, scale=-1.0).then_inc(slot.taken, 1)

                def sum_squares(use, n, semaphore):
                    slot = slots[use]
                    slot.filled(act, row, use)
                    for i in range(NB):
                        last = act.activation(sq[:, i, :], slot.tile[:, i * P:(i + 1) * P], ACT.Square,
                                              accum_out=ssum[:, n, i:i + 1])
                    last.then_inc(semaphore, 1)

                def experts_tokens():
                    draw("sum", expertsT[:], slot=SUM)
                    if layer == 0:
                        sum_squares("experts_tok", 1, sumsq_experts)
                    else:
                        slot = front["experts_tok"]
                        slot.filled(act, row, "experts_tok")
                        act.activation(gate_tanh[:], slot.tile[:], ACT.Tanh, scale=0.5).then_inc(gate_ready, 1)

                def exponentials(g, u):
                    if u == 0 and g >= 2:
                        OUT.filled(act, row, ("values", g - 2))
                    slot = back[("exp", g, u)]
                    slot.filled(act, row, ("exp", g, u))
                    act.activation(probs[:, g % 2, u, :], slot.tile[:], ACT.Exp).then_inc(slot.taken, 1)

                def state_exponentials():
                    for n in range(2):
                        act.wait_ge(expo_args, row * 2 + n + 1)
                        act.activation(expo[:, 2 * n:2 * n + 2, :], expo[:, 2 * n:2 * n + 2, :], ACT.Exp)\
                            .then_inc(expo_ready, 1)

                def ffn_tokens():
                    draw("ffn_sum", ffnT[:], slot=OUT)
                    sum_squares("ffn_tok", 2, sumsq_back)

                def end():
                    if layer == 0:
                        act.wait_ge(pre_ready, row + 1)
                        act.activation(gate[:], pre[:], ACT.Tanh, scale=0.5).then_inc(gate_ready, 1)
                    act.wait_ge(out_ready, row + 1)
                    act.dma_start(out_rows[row], x_out[:]).then_inc(out_stored, 16)

                if stage == "front":
                    return {"xnT": lambda: draw("xnT", xnT[:, 1:]), "qk": queries_keys, "router": router_exp,
                            "weights": weights, "unit": tanh_unit, "v": draw_values, "max_rows": max_rows,
                            "rwkv_proj": time_mix_draw, "experts_tok": experts_tokens}
                return {"exp": exponentials, "time_mix": state_exponentials,
                        "values": lambda g: draw(("values", g), attnU[:, g % 2, :], slot=OUT),
                        "attnT": lambda: draw("attnT", attnT[:]),
                        "oproj": lambda: sum_squares("oproj", 0, sumsq_back), "hT": lambda: draw("hT", hT[:]),
                        "ffn": tanh_ffn, "ffn_tok": ffn_tokens, "end": end}

            all_rows(act, steps_of)
            act.wait_ge(out_stored, 16 * B + 16)

        @block.gpsimd
        def _(pool):
            pool.wait_ge(weights_loaded, 16 * len(loads))
            pool.wait_ge(setup_done, 1)

            def steps_of(stage, row):
                link, count = chain(pool, f"pool_{stage}", pool_front_step if stage == "front" else pool_back_step, row)

                def inverse_root(dst, src, factor):
                    stand(pool)
                    link(pool.tensor_scalar(ssum_e[:], src, factor, EPS, ALU.mult, ALU.add))
                    return pool.tensor_tensor(dst, ssum_e[:], minus_half[:], ALU.pow)

                def norm():
                    pool.wait_ge(var_ready, row + 1)
                    inverse_root(rstd[:], meanvar[:, :, 1], 1.0).then_inc(rstd_ready, 1)

                def shifted_mix():
                    front["xnT"].drawn(pool, row, "xnT")
                    later(row, pool, front["rr"].full,
                          (row - 1) * front["rr"].per_row + front["rr"].uses.index("rr") + 1)
                    for n in range(3):
                        stand(pool)
                        pool.tensor_scalar(mix_a[:], xnT[:, 0:T], omix[:, n:n + 1], 0.0, ALU.mult, ALU.add)
                        link(pool.tensor_scalar(mix_b[:], xnT[:, 1:], cols[:, 2 + n:3 + n], 0.0, ALU.mult, ALU.add))
                        pool.tensor_tensor(mix[:, n, :], mix_b[:], mix_a[:], ALU.add).then_inc(mix_ready, 1)
                        pool.wait_ge(mix_ready, row * 3 + n + 1)

                def experts_rms():
                    if layer == 0:
                        pool.wait_ge(sumsq_experts, row + 1)
                        inverse_root(rms[:, 1, :], ssum[:, 1, :], 1.0 / C).then_inc(rms_experts, 1)
                    assert count[0] == STEPS[f"pool_{stage}"], f"pool_front {count[0]}"

                def back_rms(n):
                    pool.wait_ge(sumsq_back, row * 2 + (1, 0, 2)[n])
                    inverse_root(rms[:, n, :], ssum[:, n, :], 1.0 / C).then_inc(rms_back, 1)

                if stage == "front":
                    return {"norm": norm, "mix": shifted_mix, "experts_tok": experts_rms}
                return {"oproj": lambda: back_rms(0), "ffn_tok": lambda: back_rms(2)}

            all_rows(pool, steps_of)

        @block.vector
        def _(dve):
            for slot in (*front_slots, *back_slots, SUM, OUT):
                dve.sem_inc(slot.taken, 1)
            dve.sem_inc(out_stored, 16)
            dve.memset(K[:], 1.0)
            dve.memset(V[:], 0.0).then_inc(v_cleared, 1)
            dve.wait_ge(v_cleared, 1)
            dve.memset(V[:, :, :, DV:DV + 1], 1.0)
            dve.memset(minus_half[:], -0.5)
            dve.memset(taken[:], 0.0)
            dve.memset(w_parts[:], 0.0)
            dve.memset(max_parts[:], 0.0)
            dve.memset(xnT[:, 0:1], 0.0)
            dve.memset(onesb[:], 1.0)
            if layer == 0:
                dve.memset(o_all[:, 0:1], NEG)
                dve.memset(p_all[:, 0:1], 0.0)
                dve.memset(q_all[:, 0:1], 0.0)
            dve.wait_ge(weights_loaded, 16 * len(loads))
            dve.tensor_copy(identb[:], ident[:])
            for dst, wide in narrow:
                dve.tensor_copy(dst, wide)
            if layer == 0:
                dve.tensor_scalar(omix[:], cols[:, 2:5], -1.0, 1.0, ALU.mult, ALU.add)
                dve.wait_ge(decay_exp, 1)
                last = dve.tensor_scalar(decay[:], decay[:], -1.0, None, ALU.mult)
            else:
                dve.scalar_tensor_tensor(out=q_scale1[:], in0=scale_dims[:, 0:1], scalar=scale[:],
                                         in1=scale_dims[:, 1:2], op0=ALU.mult, op1=ALU.add)
                dve.wait_ge(direction_product, 1)
                last = dve.tensor_copy(wqk4[:].rearrange("p t d -> p (t d)"), front_slots[0].tile[:, 0:64])
            last.then_inc(setup_done, 1)
            dve.wait_ge(setup_done, 1)

            def steps_of(stage, row):
                slots = front if stage == "front" else back
                link, count = chain(dve, f"dve_{stage}", dve_front_step if stage == "front" else dve_back_step, row)

                def layer_norm():
                    dve.wait_ge(x_loaded, row * 16 + 16)
                    for i in range(NB):
                        last = dve.bn_stats(stats[:, i, :], x_in[:, i, :])
                    link(last)
                    stand(dve)
                    for i in range(NB):
                        last = dve.bn_aggr(meanvar[:, i, :], stats[:, i, :])
                    last.then_inc(var_ready, 1)
                    dve.wait_ge(var_ready, row + 1)
                    dve.wait_ge(rstd_ready, row + 1)
                    for i in range(NB):
                        last = dve.tensor_scalar(xn[:, i, :], x_in[:, i, :], meanvar[:, i, 0:1], rstd[:, i:i + 1],
                                                 ALU.subtract, ALU.mult)
                    last.then_inc(xn_ready, 1)

                def split(dst, value, rest, sign=1.0):
                    link(dve.tensor_scalar(dst(0), value, sign, None, ALU.mult))
                    link(dve.scalar_tensor_tensor(out=rest, in0=value, scalar=sign, in1=dst(0),
                                                  op0=ALU.mult, op1=ALU.subtract))
                    link(dve.tensor_copy(dst(1), rest))
                    link(dve.tensor_tensor(rest, rest, dst(1), ALU.subtract))
                    return dve.tensor_copy(dst(2), rest)

                def split_queries():
                    rows = (P, 32)[layer]
                    front["k"].drawn(dve, row, "k")
                    front["q"].drawn(dve, row, "q")
                    split(lambda s: parts[0:rows, :, s, :], compact[0:rows], split_rest[0:rows])\
                        .then_inc(parts_ready, 1)

                lg, pr, ex = logits[:, :, 0:E], pri[:, :, 0:E], expl[:, :, 0:E]

                def wide(col):
                    return top[:, :, col:col + 1].to_broadcast([P, NB, E])

                def router_choice():
                    slot = front["router"]
                    slot.filled(dve, row, "router")
                    dve.tensor_copy(lg, slot.tile[:, 0:NB * E].rearrange("p (i e) -> p i e", e=E)).then_inc(slot.taken, 1)
                    slot.drawn(dve, row, "router")
                    for k in range(2):
                        link(dve.tensor_reduce(top[:, :, 0:1], lg, AX.X, ALU.max))
                        if k == 0:
                            dve.tensor_tensor(ex, lg, wide(0), ALU.subtract).then_inc(logits_shifted, 1)
                        link(dve.tensor_tensor(pr, lg, wide(0), ALU.is_equal))
                        link(dve.tensor_tensor(pr, pr, ramp[:, :, 0:E], ALU.mult))
                        link(dve.tensor_reduce(top[:, :, 1:2], pr, AX.X, ALU.max))
                        link(dve.tensor_tensor(first[:, :, k, 0:E], pr, wide(1), ALU.is_equal))
                        if k == 0:
                            link(dve.scalar_tensor_tensor(out=lg, in0=first[:, :, 0, 0:E], scalar=NEG, in1=lg,
                                                          op0=ALU.mult, op1=ALU.add))
                    if layer == 1:
                        dve.tensor_copy(firstb[:], first[:]).then_inc(choice_ready, 1)
                    dve.wait_ge(expl_ready, row + 1)
                    link(dve.tensor_reduce(top[:, :, 2:3], ex, AX.X, ALU.add))
                    link(dve.reciprocal(top[:, :, 3:4], top[:, :, 2:3]))
                    link(dve.tensor_tensor(ex, ex, wide(3), ALU.mult))
                    if layer == 0:
                        choice_weights()

                def choice_weights():
                    link(dve.tensor_tensor(pr, first[:, :, 0, 0:E], first[:, :, 1, 0:E], ALU.add))
                    link(dve.tensor_tensor(wtop[:, :, 0:E], pr, ex, ALU.mult))
                    split(lambda s: w_parts[:, :, s, 0:E], wtop[:, :, 0:E], w_rest[:, :, 0:E])\
                        .then_inc(w_parts_ready, 1)

                def keep_ranked():
                    slot = front["rank"]
                    slot.filled(dve, row, "rank")
                    taken_row = taken[:].rearrange("p (o k) e -> p o (k e)", o=1)
                    link(dve.tensor_tensor(rank[:].rearrange("p i k e -> p i (k e)"),
                                           slot.tile[:, 0:NB * 32].rearrange("p (i n) -> p i n", i=NB),
                                           taken_row.to_broadcast([P, NB, 32]), ALU.add))
                    dve.tensor_tensor(taken[:].rearrange("p k e -> p (k e)"), slot.tile[:, NB * 32:(NB + 1) * 32],
                                      taken[:].rearrange("p k e -> p (k e)"), ALU.add).then_inc(slot.taken, 1)
                    link(dve.scalar_tensor_tensor(out=first[:].rearrange("p i k e -> p (i k e)"),
                                                  in0=rank[:].rearrange("p i k e -> p (i k e)"), scalar=capacity,
                                                  in1=first[:].rearrange("p i k e -> p (i k e)"),
                                                  op0=ALU.is_lt, op1=ALU.mult))
                    choice_weights()

                def expert_unit(e):
                    gate_slot, up, weight = front[("gate", e)], front[("up", e)], front[("weight", e)]
                    t = tanh_e[:, e % 2, :]
                    dve.wait_ge(tanh_e_ready, row * E + e + 1)
                    dve.scalar_tensor_tensor(out=t, in0=t, scalar=1.0, in1=gate_slot.tile[:], op0=ALU.add, op1=ALU.mult)\
                        .then_inc(gate_slot.taken, 1)
                    up.filled(dve, row, ("up", e))
                    gate_slot.drawn(dve, row, ("gate", e))
                    dve.scalar_tensor_tensor(out=t, in0=t, scalar=0.5, in1=up.tile[:], op0=ALU.mult, op1=ALU.mult)\
                        .then_inc(up.taken, 1)
                    if e:
                        expert_hidden(e)

                def expert_hidden(e):
                    up, weight = front[("up", e)], front[("weight", e)]
                    if e >= 2:
                        dve.wait_ge(hidden_e_used, row * (E - 1) + e - 1)
                    up.drawn(dve, row, ("up", e))
                    weight.filled(dve, row, ("weight", e))
                    dve.tensor_tensor(hidden_e[:, e % 2, :], tanh_e[:, e % 2, :], weight.tile[:], ALU.mult)\
                        .then_inc(weight.taken, 1)

                def max_unit(n):
                    i, h0, heads = max_units(H)[n]
                    slot = front[("max", n)]
                    slot.filled(dve, row, ("max", n))
                    src = slot.tile[:].rearrange("p (c k) -> p c k", c=heads)
                    dve.tensor_reduce(row_max[:, i, h0:h0 + heads], src[:, :, 0:(i + 1) * P], AX.X, ALU.max)\
                        .then_inc(slot.taken, 1)

                def max_rows():
                    n = len(max_units(H))
                    for use in [("max", m) for m in range(n - 3, n)]:
                        front[use].drawn(dve, row, use)
                    split(lambda s: max_parts[:, :, s, 0:H], row_max[:, :, 0:H], max_rest[:, :, 0:H], -1.0)\
                        .then_inc(max_parts_ready, 1)

                def rms_scaled(dst, use, n, norm, ready, value):
                    slot = slots[use]
                    slot.filled(dve, row, use)
                    dve.wait_ge(ready, value)
                    for i in range(NB):
                        last = dve.scalar_tensor_tensor(out=dst[:, i, :], in0=slot.tile[:, i * P:(i + 1) * P],
                                                        scalar=rms[:, n, i:i + 1], in1=norms[:, norm, :],
                                                        op0=ALU.mult, op1=ALU.mult)
                    last.then_inc(slot.taken, 1)
                    slot.drawn(dve, row, use)

                def experts_tokens():
                    if layer == 0:
                        rms_scaled(experts, "experts_tok", 1, 2, rms_experts, row + 1)
                    else:
                        slot = front["experts_tok"]
                        dve.wait_ge(gate_ready, row + 1)
                        dve.scalar_tensor_tensor(out=experts[:].rearrange("p i c -> p (i c)"), in0=gate_tanh[:],
                                                 scalar=1.0, in1=slot.tile[:], op0=ALU.add, op1=ALU.mult)\
                            .then_inc(slot.taken, 1)
                        slot.drawn(dve, row, "experts_tok")
                    assert count[0] == STEPS[f"dve_{stage}"], f"dve_front {count[0]}"

                def normalise_attention(g):
                    slot = back[("turn", g)]
                    slot.filled(dve, row, ("turn", g))
                    src = slot.tile[:].rearrange("p (i c d) -> p i c d", i=NB, c=4)
                    if g:
                        back[("turn", g - 1)].drawn(dve, row, ("turn", g - 1))
                    link(dve.reciprocal(rsum[:], src[:, :, :, DV]))
                    dst = attn[:, :, 4 * g * DV:4 * (g + 1) * DV].rearrange("p i (c d) -> p i c d", c=4)
                    dve.tensor_tensor(dst, src[:, :, :, 0:DV], rsum[:].unsqueeze(3).to_broadcast([P, NB, 4, DV]), ALU.mult)\
                        .then_inc(slot.taken, 1)
                    if g == G - 1:
                        slot.drawn(dve, row, ("turn", g))
                        dve.sem_inc(attn_ready, 1)

                def time_mix_states():
                    k, u, w = kv[:, 0, :], cols[:, 1:2], decay[:]
                    o_before, o_now = o_all[:, 0:T], o_all[:, 1:]
                    for use in ("rk", "rv", "rr"):
                        front[use].drawn(dve, row, use)
                    link(dve.tensor_tensor_scan(o_now, w.to_broadcast([P, T]), k, NEG, ALU.add, ALU.max))
                    dve.scalar_tensor_tensor(out=expo[:, 0, :], in0=o_before, scalar=w, in1=o_now,
                                             op0=ALU.add, op1=ALU.subtract)
                    dve.tensor_tensor(expo[:, 1, :], k, o_now, ALU.subtract).then_inc(expo_args, 1)
                    link(dve.scalar_tensor_tensor(out=t1[:], in0=k, scalar=u, in1=o_before, op0=ALU.add, op1=ALU.max))
                    dve.tensor_tensor(expo[:, 2, :], o_before, t1[:], ALU.subtract)
                    dve.scalar_tensor_tensor(out=expo[:, 3, :], in0=k, scalar=u, in1=t1[:],
                                             op0=ALU.add, op1=ALU.subtract).then_inc(expo_args, 1)

                def time_mix_result():
                    v = kv[:, 1, :]
                    dve.wait_ge(expo_ready, row * 2 + 1)
                    dve.wait_ge(expo_args, row * 2 + 2)
                    link(dve.tensor_tensor(t1[:], expo[:, 1, :], v, ALU.mult))
                    dve.tensor_tensor_scan(q_all[:, 1:], expo[:, 0, :], expo[:, 1, :], 0.0, ALU.mult, ALU.add)
                    link(dve.tensor_tensor_scan(p_all[:, 1:], expo[:, 0, :], t1[:], 0.0, ALU.mult, ALU.add))
                    dve.wait_ge(expo_ready, row * 2 + 2)
                    dve.tensor_tensor(t2[:], expo[:, 2, :], p_all[:, 0:T], ALU.mult)
                    dve.tensor_tensor(expo[:, 0, :], expo[:, 2, :], q_all[:, 0:T], ALU.mult)
                    link(dve.tensor_tensor(t1[:], expo[:, 3, :], v, ALU.mult))
                    link(dve.tensor_tensor(expo[:, 0, :], expo[:, 0, :], expo[:, 3, :], ALU.add))
                    link(dve.tensor_tensor(t1[:], t1[:], t2[:], ALU.add))
                    link(dve.scalar_tensor_tensor(out=expo[:, 0, :], in0=er[:], scalar=1.0, in1=expo[:, 0, :],
                                                  op0=ALU.add, op1=ALU.mult))
                    link(dve.reciprocal(t2[:], expo[:, 0, :]))
                    dve.tensor_tensor(rwkvT[:], t1[:], t2[:], ALU.mult).then_inc(rwkv_ready, 1)

                def attention_residual():
                    rms_scaled(tok_a, "oproj", 0, 0, rms_back, row * 2 + 1)
                    dve.tensor_tensor(hres[:], tok_a[:], xn_kept[:], ALU.add).then_inc(h_ready, 1)
                    dve.wait_ge(h_ready, row + 1)
                    link(dve.tensor_tensor(pre[:], hres[:], experts[:], ALU.add))

                def ffn_unit(f):
                    gate_slot, up = back[("gate", f)], back[("up", f)]
                    t = tanh_f[:, f % 2, :]
                    dve.wait_ge(tanh_f_ready, row * NF + f + 1)
                    dve.scalar_tensor_tensor(out=t, in0=t, scalar=1.0, in1=gate_slot.tile[:], op0=ALU.add, op1=ALU.mult)\
                        .then_inc(gate_slot.taken, 1)
                    up.filled(dve, row, ("up", f))
                    gate_slot.drawn(dve, row, ("gate", f))
                    dve.scalar_tensor_tensor(out=t, in0=t, scalar=0.5, in1=up.tile[:], op0=ALU.mult, op1=ALU.mult)\
                        .then_inc(up.taken, 1)

                def ffn_tokens():
                    rms_scaled(tok_a, "ffn_tok", 2, 1, rms_back, row * 2 + 2)
                    dve.tensor_tensor(pre[:], pre[:], tok_a[:], ALU.add).then_inc(pre_ready, 1)
                    dve.wait_ge(pre_ready, row + 1)

                def end():
                    if layer == 0:
                        g = gate[:].rearrange("p i c -> p (i c)")
                        dve.wait_ge(gate_ready, row + 1)
                        link(dve.scalar_tensor_tensor(out=gate[:], in0=gate[:], scalar=1.0, in1=pre[:],
                                                      op0=ALU.add, op1=ALU.mult))
                    else:
                        g = experts[:].rearrange("p i c -> p (i c)")
                    slot = back["s"]
                    slot.filled(dve, row, "s")
                    dve.wait_ge(out_stored, row * 16 + 16)
                    dve.scalar_tensor_tensor(out=x_out[:].rearrange("p i c -> p (i c)"), in0=g, scalar=0.5,
                                             in1=slot.tile[:], op0=ALU.mult, op1=ALU.mult).then_inc(slot.taken, 1)
                    slot.drawn(dve, row, "s")
                    dve.wait_ge(res_loaded, row * 16 + 16)
                    dve.tensor_tensor(x_out[:], x_out[:], x_res[:], ALU.add).then_inc(out_ready, 1)
                    assert count[0] == STEPS[f"dve_{stage}"], f"dve_back {count[0]}"

                if stage == "front":
                    def weights():
                        expert_hidden(0)

                    return {"norm": layer_norm, "split": split_queries, "router": router_choice, "rank": keep_ranked,
                            "unit": expert_unit, "weights": weights, "max": max_unit, "max_split": max_rows,
                            "experts_tok": experts_tokens}
                return {**({"keep": lambda: link(dve.tensor_copy(xn_kept[:], xn[:]))} if layer == 0 else {}),
                        "states": time_mix_states, "time_mix": time_mix_result, "turn": normalise_attention,
                        "oproj": attention_residual, "ffn": ffn_unit, "ffn_tok": ffn_tokens, "end": end}

            all_rows(dve, steps_of)


def build(nc, a, out):
    B, T, _ = a["x"].shape
    experts = a["gate_w"].shape[0]
    capacity = float(max(1, -(-(B * T * 2 * 5) // (experts * 4))))
    between = nc.dram_tensor("between", list(a["x"].shape), F32, kind="Internal").ap()
    build_layer(nc, a, 0, a["x"], between, capacity)
    build_layer(nc, a, 1, between, out, capacity)


def shape_constants():
    import itertools

    n = np.arange(P)
    pick = np.zeros((48, 16, P), np.float32)
    for e in range(16):
        pick[[e, 16 + e, 32 + e], e, :] = 1
    dirs = np.array(list(itertools.product([-1.0, 1.0], repeat=3)), dtype=np.float32)
    dirs = dirs / np.linalg.norm(dirs, axis=1, keepdims=True)
    m4 = np.zeros((24, 2, 4, 4), np.float32)
    for h in range(8):
        for d in range(3):
            m4[3 * h + d, h // 4, d, h % 4] = 1
            m4[3 * h + d, h // 4, 3, h % 4] = dirs[h, d]
    scaled = np.tile((np.arange(4) < 3).astype(np.float32).repeat(4), 2)
    return {
        "ident": np.eye(P, dtype=np.float32),
        "future_key": np.where(n[None, :] > n[:, None], NEG, 0).astype(np.float32),
        "past_query": np.where(n[None, :] < n[:, None], NEG, 0).astype(np.float32),
        "earlier": (n[:, None] < n[None, :]).astype(np.float32),
        "pick": pick.reshape(48, 16 * P),
        "ramp": np.broadcast_to(16 - np.arange(16, dtype=np.float32), (P, 4, 16)).copy(),
        "m4": m4.reshape(24, 32),
        "scale_dims": np.stack([scaled, 1 - scaled], 1),
    }


def kernel(**inputs):
    import concourse.bacc as bacc
    from concourse.bass_utils import run_bass_kernel_spmd

    x = {k: np.asarray(v) for k, v in inputs.items()}
    L0, L1 = "L0_attn_", "L1_attn_"

    def by_dim(w):
        return np.ascontiguousarray(w.reshape(P, 2, 8, 8).transpose(0, 1, 3, 2).reshape(P, P))

    arrays = {
        "x": x[L0 + "x"],
        "wq": by_dim(x["L0_ffn_wq"]), "wk": by_dim(x["L0_ffn_wk"]), "wv": x["L0_ffn_wv"], "wo": x["L0_ffn_wo"],
        "rk": x[L0 + "Wk"].T, "rv": x[L0 + "Wv"].T, "rr": x[L0 + "Wr"].T, "ro": x[L0 + "Wo"].T,
        "w1": x["L0_ffn_w1"], "w3": x["L0_ffn_w3"], "w2": x["L0_ffn_w2"],
        "router0": x["L0_ffn_router_w"], "ew1": x["L0_ffn_ew1"], "ew2": x["L0_ffn_ew2"], "ew3": x["L0_ffn_ew3"],
        "Wq1": x[L1 + "Wq"], "Wk1": x[L1 + "Wk"], "v1w": x[L1 + "Wv"].T, "o1w": x[L1 + "Wo"].T,
        "scale": x[L1 + "scale"].reshape(1, 1),
        "router1": x["L1_ffn_router_w"], "gate_w": x["L1_ffn_gate_w"], "up_w": x["L1_ffn_up_w"],
        "down_w": x["L1_ffn_down_w"],
        **{n: x[L0 + n] for n in ("time_decay", "time_first")},
        **{n: x[L0 + n].reshape(P) for n in ("time_mix_k", "time_mix_v", "time_mix_r")},
        **{n: x["L0_ffn_" + n] for n in ("attn_norm_w", "ff_norm_w", "moe_norm_w")},
        **shape_constants(),
    }
    nc = bacc.Bacc("TRN2", target_bir_lowering=False, num_devices=1)
    arrays = {f"in_{k}": np.ascontiguousarray(v) for k, v in arrays.items()}
    args = {k[3:]: nc.dram_tensor(k, v.shape, mybir.dt.from_np(v.dtype), kind="ExternalInput").ap()
            for k, v in arrays.items()}
    out = nc.dram_tensor("out_0", x[L0 + "x"].shape, F32, kind="ExternalOutput").ap()
    build(nc, args, out)
    r = run_bass_kernel_spmd(nc, [arrays], core_ids=[0])
    return r.results[0]["out_0"]
```

```python
from contextlib import ExitStack

import numpy as np

import concourse.bass as bass
import concourse.mybir as mybir

F32 = mybir.dt.float32
BF16 = mybir.dt.bfloat16
ALU = mybir.AluOpType
ACT = mybir.ActivationFunctionType
AX = mybir.AxisListType

P = 128
EPS = 1e-5
NEG = -1e38

Q_RUNS = [(0, 3, 0, 0), (3, 2, 1, 0), (5, 1, 2, 0)]
K_RUNS = [(0, 3, 0, 1), (3, 2, 0, 1), (5, 1, 0, 0)]
COPIES, PARTS = 6, 3
STACK_DMAS = 12
LEAD = (2, 3)


class Slot:

    def __init__(self, tile, full, taken, uses):
        self.tile, self.full, self.taken, self.uses = tile, full, taken, list(uses)
        self.per_row = len(self.uses)

    def claim(self, pe, row, use):
        pe.wait_ge(self.taken, row * self.per_row + self.uses.index(use) + 1)

    def filled(self, eng, row, use):
        eng.wait_ge(self.full, row * self.per_row + self.uses.index(use) + 1)

    def drawn(self, eng, row, use):
        eng.wait_ge(self.taken, row * self.per_row + self.uses.index(use) + 2)


def max_units(heads):
    out = []
    for i, n in ((3, 1), (2, 1), (1, 2), (0, 4)):
        out += [(i, h, n) for h in range(0, heads, n)]
    return out


PACE = ({"norm": 50, "xnT": 14, "qk": 20, "router": 20, "weights": 15, "unit": 32, "down": 9, "split": 5,
         "stacks": 1.5, "v": 9, "max": 6, "max_split": 1.4, "max_rows": 10, "rwkv_proj": 46.8, "max_load": 5,
         "exp": 9, "values": 30, "turn": 10, "attnT": 15, "oproj": 60, "hT": 45, "ffn": 15, "ffn_down": 9,
         "ffn_tok": 40, "s": 2.7, "end": 20, "maxima": 10, "experts_tok": 1},
        {"norm": 50, "xnT": 21, "qk": 20, "router": 20, "rank": 30, "weights": 15, "unit": 32, "down": 9,
         "split": 15.8, "stacks": 5, "v": 9, "max": 12, "max_split": 4, "max_rows": 20, "max_load": 5,
         "exp": 4.2, "values": 30, "turn": 10, "attnT": 7.5, "s": 13.5, "end": 20, "maxima": 20,
         "experts_tok": 1.4})
SHAPE = (dict(beside=5, before=2, after=1, early=2, states_after=1),
         dict(beside=7, before=0, after=3, early=2, states_after=0))


def merged(pace, front, back):
    out, done = [], [0, 0]
    lists = [list(front), list(back)]
    total = [sum(pace.get(step[0], 2) for step in x) for x in lists]
    while any(lists):
        side = min((n for n in range(2) if lists[n]), key=lambda n: done[n] / total[n])
        step = lists[side].pop(0)
        out.append((("front", "back")[side], step))
        done[side] += pace.get(step[0], 2)
    return out


def spread(steps, among):
    out, at = [], 0
    for n, x in enumerate(among):
        out.append(x)
        while at < len(steps) and (at + 1) * len(among) <= (n + 1) * len(steps):
            out.append(steps[at])
            at += 1
    return out


def plan_of(layer, heads, experts, ffn_units):
    groups = heads // 4

    def units(e0, e1):
        out = []
        for e in range(e0, e1):
            out += [("unit", e), ("down", e - 1)]
        return out

    beside, before, after, early, states_after = SHAPE[layer].values()
    maxima_from, maxima_to = beside + before, experts - after
    front_a = [("xnT",), ("router",), ("qk",), ("split",), *[("unit", e) for e in range(LEAD[layer])]]
    front_a += ([("rank",)] if layer else []) + [("weights",)]
    front_a += ([("mix",)] if layer == 0 else []) + [("down", e) for e in range(LEAD[layer] - 1)]
    front_a += units(LEAD[layer], beside)
    front_b = [("stacks",), ("v",), *units(beside, maxima_from)]
    rest = units(maxima_from, maxima_to)
    front_b += spread(rest, [("max", n) for n in range(len(max_units(heads)))]) + [("max_split",)]
    last_units = units(maxima_to, experts)
    front_b += last_units[:early] + [("keep",), ("norm",), ("max_rows",)] + last_units[early:]
    front_b += ([("rwkv_proj",)] if layer == 0 else []) + [("down", experts - 1), ("max_load",)]

    time_mix = iter([("time_mix",), ("time_mix2",), ("time_mix3",)] if layer == 0 else [])
    back_a = [("maxima",)]
    for g in range(groups + 1):
        if g < groups:
            back_a += [("exp", g, u) for u in range(5)]
        if g == 0:
            back_a += [("experts_tok",)]
        if g == states_after and layer == 0:
            back_a.append(("states",))
        if g >= 2:
            back_a.append(("turn", g - 2))
        if g >= 1 + states_after:
            back_a += [x for x in (next(time_mix, None),) if x]
        if g < groups:
            back_a += [("exp", g, u) for u in range(5, 10)]
        if g >= 1:
            back_a.append(("values", g - 1))
    back_b = [("turn", groups - 1), ("attnT",)]
    if layer == 0:
        back_b += [("oproj",), ("hT",)]
        for f in range(ffn_units):
            back_b.append(("ffn", f))
            if f:
                back_b.append(("ffn_down", f - 1))
        back_b += [("ffn_down", ffn_units - 1), ("ffn_tok",)]
    back_b += [("s",), ("end",)]
    order = [("back", ("residual",))] + merged(PACE[layer], front_a, back_a) + merged(PACE[layer], front_b, back_b)
    order = [(stage, step) for stage, step in order if step != ("maxima",)]
    return [("next", step) if step == ("norm",) else (stage, step) for stage, step in order]


def step_uses(layer, step):
    name, n = step[0], step[1:]
    return {
        "xnT": ["xnT"], "qk": ["q", "k"], "router": ["router"], "rank": ["rank"],
        "weights": ["weights"] + [("weight", e) for e in range(LEAD[layer])],
        "unit": [("gate", *n), ("up", *n)] + ([("weight", *n)] if n and n[0] >= LEAD[layer] else []),
        "v": ["v"], "max": [("max", *n)], "max_rows": ["max_rows"],
        "rwkv_proj": ["rk", "rv", "rr"], "experts_tok": ["experts_tok"],
        "exp": [("exp", *n)], "turn": [("turn", *n)], "attnT": ["attnT"], "oproj": ["oproj"], "hT": ["hT"],
        "ffn": [("gate", *n), ("up", *n)], "ffn_tok": ["ffn_tok"], "s": ["s"],
    }.get(name, [])


def build_layer(nc, a, layer, x_src, x_dst, capacity):
    B, T, C = x_src.shape
    NB = T // P
    H = (16, 8)[layer]
    D = (8, 4)[layer]
    DV = P // H
    J = H // 2
    G = H // 4
    ROWS = H * D
    E = a[("ew1", "gate_w")[layer]].shape[0]
    FF = a["w1"].shape[1]
    NF = FF // P
    plan = plan_of(layer, H, E, NF)
    by_tanh = SHAPE[layer]["beside"]

    with ExitStack() as ctx:
        def sb(name, shape, dt=F32):
            return ctx.enter_context(nc.sbuf_tensor(f"{name}_{layer}", shape, dt))

        def sem(name):
            return ctx.enter_context(nc.semaphore(f"{name}_{layer}"))

        ident = sb("ident", [P, P])
        identb = sb("identb", [P, P], BF16)
        future_key = sb("future_key", [P, P], BF16)
        past_query = sb("past_query", [P, P], BF16)
        earlier = sb("earlier", [P, P], BF16)
        onesb = sb("onesb", [P, P], BF16)
        pick = sb("pick", [48, 16, P], BF16)
        ramp = sb("ramp", [P, NB, 16])
        wv = sb("wv", [P, P])
        router = sb("router", [P, E])
        we_gate, we_up, we_down = (sb(n, [P, E, P]) for n in ("we_gate", "we_up", "we_down"))
        minus_half = sb("minus_half", [P, NB])
        if layer == 0:
            wq, wk, wo = (sb(n, [P, P]) for n in ("wq", "wk", "wo"))
            rk, rv, rr, ro = (sb(n, [P, P]) for n in ("rk", "rv", "rr", "ro"))
            w1, w3, w2 = sb("w1", [P, FF]), sb("w3", [P, FF]), sb("w2", [P, NF, P])
            norms = sb("norms", [P, 3, C])
            cols = sb("cols", [P, 5])
            decay = sb("decay", [P, 1])
            omix = sb("omix", [P, 3])
        else:
            m4 = sb("m4", [24, 32])
            wqk3 = sb("wqk3", [24, 2, P])
            wqk4 = sb("wqk4", [P, 2, 32])
            o1w = sb("o1w", [P, P])
            scale = sb("scale", [32, 1])
            scale_dims = sb("scale_dims", [32, 2])
            q_scale1 = sb("q_scale1", [32, 1])

        x_in = sb("x_in", [P, NB, C])
        stats = sb("stats", [P, NB, 6])
        meanvar = sb("meanvar", [P, NB, 2])
        rstd = sb("rstd", [P, NB])
        xn = sb("xn", [P, NB, C])
        xnT = sb("xnT", [P, 1 + T])
        compact = sb("compact", [P, 2, T])
        split_rest = sb("split_rest", [P, 2, T])
        parts = sb("parts", [P, 2, PARTS, T], BF16)
        row_max = sb("row_max", [P, NB, 16])
        max_rest = sb("max_rest", [P, NB, 16])
        max_parts = sb("max_parts", [P, NB, PARTS, 16], BF16)
        maxT = sb("maxT", [48, T], BF16)
        logits = sb("logits", [P, NB, 16])
        pri = sb("pri", [P, NB, 16])
        first = sb("first", [P, NB, 2, 16])
        top = sb("top", [P, NB, 4])
        expl = sb("expl", [P, NB, 16])
        wtop = sb("wtop", [P, NB, 16])
        w_rest = sb("w_rest", [P, NB, 16])
        w_parts = sb("w_parts", [P, NB, PARTS, 16], BF16)
        weightT = sb("weightT", [48, T], BF16)
        firstb = sb("firstb", [P, NB, 2, 16], BF16)
        rank = sb("rank", [P, NB, 2, 16])
        taken = sb("taken", [P, 2, 16])
        gated_e = sb("gated_e", [P, LEAD[layer], T])
        hidden_e = sb("hidden_e", [P, 2, T])
        expertsT = sb("expertsT", [P, T])
        experts = sb("experts", [P, NB, C])
        sq = sb("sq", [P, NB, C])
        ssum = sb("ssum", [P, 3, NB])
        root_of = sb("root_of", [P, 4, NB])
        rms = sb("rms", [P, 3, NB])
        if layer == 0:
            mix = sb("mix", [P, 3, T])
            mix_a, mix_b = sb("mix_a", [P, T]), sb("mix_b", [P, T])
        else:
            gate_tanh = sb("gate_tanh", [P, T])

        Q = sb("q_stack", [P, J, T], BF16)
        K = sb("k_stack", [P, J, T], BF16)
        V = sb("v", [P, NB, H, 32])
        if layer == 0:
            kv = sb("kv", [P, 2, T])
            er = sb("er", [P, T])

        x_res = sb("x_res", [P, NB, C])
        probs = sb("probs", [P, 2, 10, 512])
        attnU = sb("attnU", [P, 2, T])
        rsum = sb("rsum", [P, NB, 4])
        attn = sb("attn", [P, NB, C])
        attnT = sb("attnT", [P, T])
        x_out = sb("x_out", [P, NB, C])
        if layer == 0:
            xn_kept = sb("xn_kept", [P, NB, C])
            o_all = sb("o_all", [P, 1 + T])
            p_all = sb("p_all", [P, 1 + T])
            q_all = sb("q_all", [P, 1 + T])
            expo = sb("expo", [P, 4, T])
            t1, t2 = sb("t1", [P, T]), sb("t2", [P, T])
            rwkvT = sb("rwkvT", [P, T])
            tok_a = sb("tok_a", [P, NB, C])
            hres = sb("hres", [P, NB, C])
            hT = sb("hT", [P, T])
            pre = sb("pre", [P, NB, C])
            gate = sb("gate", [P, NB, C])
            hidden_f = sb("hidden_f", [P, 2, T])
            ffnT = attnT

        qk_dram = nc.dram_tensor(f"qk_scratch{layer}", [2, PARTS, P, T], BF16, kind="Internal").ap()
        max_dram = nc.dram_tensor(f"max_scratch{layer}", [48, T], BF16, kind="Internal").ap()

        def psum(name):
            return ctx.enter_context(nc.psum_tensor(f"{name}_{layer}", [P, T], F32))

        def ring(stage):
            order = [u for where, step in plan if where == stage for u in step_uses(layer, step)]
            slots = [Slot(psum(f"{stage}{n}"), sem(f"{stage}{n}_full"), sem(f"{stage}{n}_taken"), order[n::3])
                     for n in range(3)]
            return {use: slots[n % 3] for n, use in enumerate(order)}, slots

        front, front_slots = ring("front")
        back, back_slots = ring("back")
        SUM = Slot(psum("experts_sum"), sem("experts_sum_full"), sem("experts_sum_taken"), ["sum"])
        OUT = Slot(psum("values_bank"), sem("values_bank_full"), sem("values_bank_taken"),
                   [("values", g) for g in range(G)] + ([] if layer else ["ffn_sum"]))

        weights_loaded = sem("weights_loaded")
        direction_product = sem("direction_product")
        decay_exp = sem("decay_exp")
        setup_done = sem("setup_done")
        v_cleared = sem("v_cleared")
        x_loaded = sem("x_loaded")
        res_loaded = sem("res_loaded")
        var_ready = sem("var_ready")
        rstd_ready = sem("rstd_ready")
        xn_ready = sem("xn_ready")
        parts_ready = sem("parts_ready")
        parts_stored = sem("parts_stored")
        stacks_loaded = sem("stacks_loaded")
        max_parts_ready = sem("max_parts_ready")
        max_stored = sem("max_stored")
        max_loaded = sem("max_loaded")
        logits_shifted = sem("logits_shifted")
        expl_ready = sem("expl_ready")
        choice_ready = sem("choice_ready")
        w_parts_ready = sem("w_parts_ready")
        tanh_e_ready = sem("tanh_e_ready")
        hidden_e_used = sem("hidden_e_used")
        hidden_f_used = sem("hidden_f_used")
        sumsq_experts = sem("sumsq_experts")
        sumsq_back = sem("sumsq_back")
        rms_experts = sem("rms_experts")
        rms_back = sem("rms_back")
        attn_ready = sem("attn_ready")
        h_ready = sem("h_ready")
        mix_ready = sem("mix_ready")
        expo_args = sem("expo_args")
        expo_ready = sem("expo_ready")
        rwkv_ready = sem("rwkv_ready")
        pre_ready = sem("pre_ready")
        gate_ready = sem("gate_ready")
        out_ready = sem("out_ready")
        out_stored = sem("out_stored")
        waits_met = sem("waits_met")
        dve_step = {stage: sem(f"dve_{stage}_step") for stage in ("next", "front", "back")}
        pool_step = {stage: sem(f"pool_{stage}_step") for stage in ("next", "front", "back")}
        STEPS = ({"dve_next": 1, "dve_front": 29, "dve_back": 14, "pool_next": 1, "pool_front": 3, "pool_back": 3},
                 {"dve_next": 1, "dve_front": 30, "dve_back": 2, "pool_next": 1, "pool_front": 0, "pool_back": 0})[layer]

        def stand(eng):
            eng.sem_inc(waits_met, 1)

        links = {}

        def chain(eng, name, semaphore, row):
            links[name] = count = [0]

            def link(ins):
                count[0] += 1
                ins.then_inc(semaphore, 1)
                eng.wait_ge(semaphore, row * STEPS[name] + count[0])

            return link

        def run(steps_of, rows):
            does = {stage: steps_of(stage, row) for stage, row in rows.items()}
            for stage, step in plan:
                if stage in does and step[0] in does[stage]:
                    does[stage][step[0]](*step[1:])

        def all_rows(eng, steps_of):
            run(steps_of, {"next": 0})
            run(steps_of, {"next": 1, "front": 0})
            with eng.Fori(0, B - 2) as i:
                run(steps_of, {"next": i + 2, "front": i + 1, "back": i})
            run(steps_of, {"front": B - 1, "back": B - 2})
            run(steps_of, {"back": B - 1})
            assert all(count[0] == STEPS[name] for name, count in links.items()), links

        loads = []

        def load(dst, src):
            loads.append((dst, src))

        wide_room = probs[:].rearrange("p g u t -> p (g u t)")
        narrow = [(future_key[:], wide_room[:, 0:P]), (past_query[:], wide_room[:, P:2 * P]),
                  (earlier[:], wide_room[:, 2 * P:3 * P]),
                  (pick[:].rearrange("p e n -> p (e n)"), wide_room[0:48, 4 * P:20 * P])]
        for (_, wide), src in zip(narrow, ("future_key", "past_query", "earlier", "pick")):
            load(wide, a[src])
        load(ident[:], a["ident"])
        load(ramp[:], a["ramp"])
        for dst, src in zip((we_gate, we_up, we_down), (("ew1", "ew3", "ew2"), ("gate_w", "up_w", "down_w"))[layer]):
            load(dst[:], a[src].rearrange("e p h -> p e h"))
        if layer == 0:
            for dst, src in ((wq, "wq"), (wk, "wk"), (wv, "wv"), (wo, "wo"), (rk, "rk"), (rv, "rv"), (rr, "rr"),
                             (ro, "ro"), (w1, "w1"), (w3, "w3"), (router, "router0")):
                load(dst[:], a[src])
            load(w2[:], a["w2"].rearrange("(f p) d -> p f d", p=P))
            for n, src in enumerate(("attn_norm_w", "ff_norm_w", "moe_norm_w")):
                load(norms[:, n, :], a[src].rearrange("(o c) -> o c", o=1).to_broadcast([P, C]))
            for n, src in enumerate(("time_decay", "time_first", "time_mix_k", "time_mix_v", "time_mix_r")):
                load(cols[:, n:n + 1], a[src].rearrange("(c o) -> c o", o=1))
        else:
            for dst, src in ((m4, "m4"), (scale_dims, "scale_dims"), (wv, "v1w"), (o1w, "o1w"), (router, "router1")):
                load(dst[:], a[src])
            load(wqk3[:, 0, :], a["Wq1"])
            load(wqk3[:, 1, :], a["Wk1"])
            load(scale[:], a["scale"].to_broadcast([32, 1]))

        x_rows = x_src.rearrange("b (i p) c -> b p i c", p=P)
        out_rows = x_dst.rearrange("b (i p) c -> b p i c", p=P)

        block = ctx.enter_context(nc.Block())

        def later(row, eng, semaphore, value):
            if not isinstance(row, int) or row > 0:
                eng.wait_ge(semaphore, value)

        @block.sync
        def _(sp):
            for dst, src in loads[0::2]:
                sp.dma_start(dst, src).then_inc(weights_loaded, 16)

            def steps_of(stage, row):
                def norm():
                    later(row, sp, xn_ready, row)
                    sp.dma_start(x_in[:], x_rows[row]).then_inc(x_loaded, 16)

                def stacks():
                    sp.wait_ge(parts_ready, row + 1)
                    for t in range(2):
                        sp.dma_start(qk_dram[t, :, 0:ROWS, :].rearrange("s p t -> p s t"),
                                     parts[0:ROWS, t]).then_inc(parts_stored, 16)
                    sp.wait_ge(parts_stored, row * 32 + 32)
                    last = ("exp", G - 1, 9)
                    later(row, sp, back[last].full, (row - 1) * back[last].per_row + back[last].uses.index(last) + 1)
                    for t, (stack, runs) in enumerate(((Q, Q_RUNS), (K, K_RUNS))):
                        for half in range(2):
                            for c0, n, part, step in runs:
                                src = qk_dram[t, part:part + (n if step else 1), half * D * J:(half + 1) * D * J, :]
                                src = src.rearrange("s (d j) t -> s d (j t)", d=D)
                                if not step and n > 1:
                                    src = src.to_broadcast([n, D, J * T])
                                p0 = 64 * half + c0 * D
                                sp.dma_start(stack[p0:p0 + n * D].rearrange("p j t -> p (j t)"), src)\
                                    .then_inc(stacks_loaded, 16)

                def max_load():
                    front["max_rows"].drawn(sp, row, "max_rows")
                    sp.dma_start(max_dram, maxT[:]).then_inc(max_stored, 16)
                    sp.wait_ge(max_stored, row * 16 + 16)
                    for half in range(2):
                        p0 = 64 * half + COPIES * D
                        src = max_dram.rearrange("(s h) t -> s h t", s=PARTS)[:, half * J:(half + 1) * J, :]
                        sp.dma_start(Q[p0:p0 + PARTS], src).then_inc(max_loaded, 16)

                def residual():
                    later(row, sp, out_ready, row)
                    sp.dma_start(x_res[:], x_rows[row]).then_inc(res_loaded, 16)

                return {"next": {"norm": norm}, "front": {"stacks": stacks, "max_load": max_load},
                        "back": {"residual": residual}}[stage]

            all_rows(sp, steps_of)

        @block.tensor
        def _(pe):
            pe.wait_ge(weights_loaded, 16 * len(loads))
            if layer == 1:
                for t in range(2):
                    mm = pe.matmul(front_slots[0].tile[:, 32 * t:32 * t + 32], wqk3[:, t, :], m4[:], start=True, stop=True)
                mm.then_inc(direction_product, 1)
            pe.wait_ge(setup_done, 1)

            def steps_of(stage, row):
                slots = front if stage == "front" else back

                def transpose_blocks(use, src):
                    slot = slots[use]
                    slot.claim(pe, row, use)
                    for i in range(NB):
                        mm = pe.transpose(slot.tile[:, i * P:(i + 1) * P], src(i), ident[:])
                    mm.then_inc(slot.full, 1)

                def parts_to_rows(use, src):
                    slot = slots[use]
                    slot.claim(pe, row, use)
                    stand(pe)
                    dst = slot.tile[:].bitcast(BF16)
                    for i in range(NB):
                        mm = pe.transpose(dst[0:48, i * P:(i + 1) * P], src[:, i].rearrange("p s e -> p (s e)"),
                                          identb[:])
                    mm.then_inc(slot.full, 1)

                def project(use, w, src, rows=P):
                    slot = slots[use]
                    slot.claim(pe, row, use)
                    pe.matmul(slot.tile[0:rows, :], w, src, start=True, stop=True).then_inc(slot.full, 1)

                def token_project(use, src, w, n=P):
                    slot = slots[use]
                    slot.claim(pe, row, use)
                    for i in range(NB):
                        mm = pe.matmul(slot.tile[:, i * n:(i + 1) * n], src(i), w, start=True, stop=True)
                    mm.then_inc(slot.full, 1)

                def xnT_block(i):
                    return xnT[:, 1 + i * P:1 + (i + 1) * P]

                def turn_norm():
                    pe.wait_ge(xn_ready, row + 1)
                    transpose_blocks("xnT", lambda i: xn[:, i, :])

                def expert_logits():
                    front["xnT"].drawn(pe, row, "xnT")
                    token_project("router", xnT_block, router[:], E)

                def queries_keys():
                    rows = (P, 32)[layer]
                    for use, w in zip("qk", ((wq[:], wk[:]) if layer == 0 else (wqk4[:, 0, :], wqk4[:, 1, :]))):
                        project(use, w, xnT[:, 1:], rows)

                def choice_ranks():
                    pe.wait_ge(choice_ready, row + 1)
                    slot = front["rank"]
                    slot.claim(pe, row, "rank")
                    for i in range(NB + 1):
                        dst = slot.tile[:, i * 32:(i + 1) * 32]
                        if i < NB:
                            pe.matmul(dst, earlier[:], firstb[:, i].rearrange("p k e -> p (k e)"),
                                      start=True, stop=(i == 0))
                        for before in range(i):
                            mm = pe.matmul(dst, onesb[:], firstb[:, before].rearrange("p k e -> p (k e)"),
                                           start=(i == NB and before == 0), stop=(before == i - 1))
                    mm.then_inc(slot.full, 1)

                def expert_weights():
                    pe.wait_ge(w_parts_ready, row + 1)
                    parts_to_rows("weights", w_parts)

                def expert_unit(e):
                    project(("gate", e), we_gate[:, e, :], xnT[:, 1:])
                    project(("up", e), we_up[:, e, :], xnT[:, 1:])

                def expert_weight(e):
                    if e == 0:
                        front["weights"].drawn(pe, row, "weights")
                    project(("weight", e), pick[:, e, :], weightT[:])

                def expert_down(e):
                    front[("weight", e)].drawn(pe, row, ("weight", e))
                    if e == 0:
                        SUM.claim(pe, row, "sum")
                    last = e == E - 1
                    pe.matmul(SUM.tile[:], we_down[:, e, :], hidden_e[:, e % 2, :], start=(e == 0), stop=last)\
                        .then_inc(SUM.full if last else hidden_e_used, 1)

                def max_unit(n):
                    if n == 0:
                        pe.wait_ge(stacks_loaded, row * 16 * STACK_DMAS + 16 * STACK_DMAS)
                    i, h0, count = max_units(H)[n]
                    slot = front[("max", n)]
                    slot.claim(pe, row, ("max", n))
                    keys = (i + 1) * P
                    for c in range(count):
                        p0, j, c0 = 64 * ((h0 + c) // J), (h0 + c) % J, c * (T // count)
                        q = Q[p0:p0 + COPIES * D, j, i * P:(i + 1) * P]
                        k = K[p0:p0 + COPIES * D, j, 0:keys]
                        pe.matmul(slot.tile[:, c0:c0 + keys], q, k, start=True, stop=False)
                        mm = pe.matmul(slot.tile[:, c0 + i * P:c0 + keys], identb[:], future_key[:],
                                       start=False, stop=True)
                    mm.then_inc(slot.full, 1)

                def max_rows():
                    pe.wait_ge(max_parts_ready, row + 1)
                    parts_to_rows("max_rows", max_parts)

                def time_mix_projections():
                    for n, (use, w) in enumerate((("rk", rk), ("rv", rv), ("rr", rr))):
                        pe.wait_ge(mix_ready, row * 3 + n + 1)
                        project(use, w[:], mix[:, n, :])

                def experts_tokens():
                    SUM.drawn(pe, row, "sum")
                    transpose_blocks("experts_tok", lambda i: expertsT[:, i * P:(i + 1) * P])

                def scores(g, u):
                    def piece(dst, h, kb):
                        p0, j = 64 * (h // J), h % J
                        rows = COPIES * D + PARTS
                        pe.matmul(dst, K[p0:p0 + rows, j, kb * P:(kb + 1) * P], Q[p0:p0 + rows, j, kb * P:T],
                                  start=True, stop=False)
                        return pe.matmul(dst[:, 0:P], identb[:], past_query[:], start=False, stop=True)

                    if (g, u) == (0, 0):
                        pe.wait_ge(max_loaded, row * 32 + 32)
                    slot = back[("exp", g, u)]
                    slot.claim(pe, row, ("exp", g, u))
                    if u < 8 and u % 2 == 0:
                        mm = piece(slot.tile[:], 4 * g + u // 2, 0)
                    elif u < 8:
                        piece(slot.tile[:, 0:384], 4 * g + u // 2, 1)
                        mm = piece(slot.tile[:, 384:512], 4 * g + u // 2, 3)
                    else:
                        for c in range(2):
                            mm = piece(slot.tile[:, 256 * c:256 * c + 256], 4 * g + 2 * (u - 8) + c, 2)
                    mm.then_inc(slot.full, 1)

                def values(g):
                    back[("exp", g, 9)].drawn(pe, row, ("exp", g, 9))
                    OUT.claim(pe, row, ("values", g))
                    pb = probs[:, g % 2]
                    for kb in (0, 1, 3, 2):
                        for c in range(4):
                            src = {0: pb[:, 2 * c, :], 1: pb[:, 2 * c + 1, 0:384], 3: pb[:, 2 * c + 1, 384:512],
                                   2: pb[:, 8 + c // 2, 256 * (c % 2):256 * (c % 2) + 256]}[kb]
                            mm = pe.matmul(OUT.tile[32 * c:32 * c + 32, kb * P:T], V[:, kb, 4 * g + c, :], src,
                                           start=(kb == 0), stop=(kb == 2), skip_group_check=True)
                    mm.then_inc(OUT.full, 1)

                def turn_values(g):
                    OUT.drawn(pe, row, ("values", g))
                    transpose_blocks(("turn", g), lambda i: attnU[:, g % 2, i * P:(i + 1) * P])

                def turn_attention():
                    pe.wait_ge(attn_ready, row + 1)
                    transpose_blocks("attnT", lambda i: attn[:, i, :])

                def out_projection():
                    back["attnT"].drawn(pe, row, "attnT")
                    token_project("oproj", lambda i: attnT[:, i * P:(i + 1) * P], wo[:])

                def turn_h():
                    pe.wait_ge(h_ready, row + 1)
                    transpose_blocks("hT", lambda i: hres[:, i, :])

                def ffn_unit(f):
                    if f == 0:
                        back["hT"].drawn(pe, row, "hT")
                    project(("gate", f), w1[:, f * P:(f + 1) * P], hT[:])
                    project(("up", f), w3[:, f * P:(f + 1) * P], hT[:])

                def ffn_down(f):
                    back[("up", f)].drawn(pe, row, ("up", f))
                    if f == 0:
                        OUT.claim(pe, row, "ffn_sum")
                    last = f == NF - 1
                    pe.matmul(OUT.tile[:], w2[:, f, :], hidden_f[:, f % 2, :], start=(f == 0), stop=last)\
                        .then_inc(OUT.full if last else hidden_f_used, 1)

                def ffn_tokens():
                    OUT.drawn(pe, row, "ffn_sum")
                    transpose_blocks("ffn_tok", lambda i: ffnT[:, i * P:(i + 1) * P])

                def branch_output():
                    if layer == 0:
                        pe.wait_ge(rwkv_ready, row + 1)
                        token_project("s", lambda i: rwkvT[:, i * P:(i + 1) * P], ro[:])
                    else:
                        back["attnT"].drawn(pe, row, "attnT")
                        token_project("s", lambda i: attnT[:, i * P:(i + 1) * P], o1w[:])

                if stage == "next":
                    return {}
                if stage == "front":
                    def unit(e):
                        expert_unit(e)
                        if e >= LEAD[layer]:
                            expert_weight(e)

                    def weights():
                        expert_weights()
                        for e in range(LEAD[layer]):
                            expert_weight(e)

                    return {"xnT": turn_norm, "qk": queries_keys,
                            "router": expert_logits,
                            "rank": choice_ranks, "weights": weights, "unit": unit, "down": expert_down,
                            "v": lambda: token_project("v", xnT_block, wv[:]), "max": max_unit, "max_rows": max_rows,
                            "rwkv_proj": time_mix_projections}
                return {"experts_tok": experts_tokens, "exp": scores, "values": values, "turn": turn_values, "attnT": turn_attention,
                        "oproj": out_projection, "hT": turn_h, "ffn": ffn_unit, "ffn_down": ffn_down,
                        "ffn_tok": ffn_tokens, "s": branch_output}

            all_rows(pe, steps_of)

        @block.scalar
        def _(act):
            for dst, src in loads[1::2]:
                act.dma_start(dst, src).then_inc(weights_loaded, 16)
            act.wait_ge(weights_loaded, 16 * len(loads))
            if layer == 0:
                act.activation(decay[:], cols[:, 0:1], ACT.Exp).then_inc(decay_exp, 1)
            act.wait_ge(setup_done, 1)

            def steps_of(stage, row):
                slots = front if stage == "front" else back

                def draw(use, dst, src=None, scale=1.0, slot=None):
                    slot = slot or slots[use]
                    slot.filled(act, row, use)
                    act.activation(dst, slot.tile[:] if src is None else src, ACT.Copy, scale=scale)\
                        .then_inc(slot.taken, 1)

                def queries_keys():
                    rows = (P, 32)[layer]
                    draw("q", compact[0:rows, 0, :], front["q"].tile[0:rows, :],
                         scale=(float(D) ** -0.5 if layer == 0 else q_scale1[:]))
                    draw("k", compact[0:rows, 1, :], front["k"].tile[0:rows, :])

                def router_exp():
                    act.wait_ge(logits_shifted, row + 1)
                    act.activation(expl[:, :, 0:E], expl[:, :, 0:E], ACT.Exp).then_inc(expl_ready, 1)

                def weights():
                    draw("weights", weightT[:], front["weights"].tile[:].bitcast(BF16)[0:48, 0:T])

                def gate_unit(e):
                    slot = slots[("gate", e)]
                    slot.filled(act, row, ("gate", e))
                    if e >= LEAD[layer]:
                        slots[("weight", e - LEAD[layer])].drawn(act, row, ("weight", e - LEAD[layer]))
                    if e < by_tanh:
                        act.activation(gated_e[:, e % LEAD[layer], :], slot.tile[:], ACT.Tanh, scale=0.5)\
                            .then_inc(tanh_e_ready, 1)
                    else:
                        act.activation(gated_e[:, e % LEAD[layer], :], slot.tile[:], ACT.Silu).then_inc(slot.taken, 1)

                def silu_ffn(f):
                    slot = slots[("gate", f)]
                    slot.filled(act, row, ("gate", f))
                    if f >= 2:
                        act.wait_ge(hidden_f_used, row * (NF - 1) + f - 1)
                    act.activation(hidden_f[:, f % 2, :], slot.tile[:], ACT.Silu).then_inc(slot.taken, 1)

                def draw_values():
                    last = ("values", G - 1)
                    later(row, act, OUT.full, (row - 1) * OUT.per_row + OUT.uses.index(last) + 1)
                    draw("v", V[:, :, :, 0:DV], front["v"].tile[:].rearrange("p (i h d) -> p i h d", i=NB, h=H))

                def max_rows():
                    draw("max_rows", maxT[:], front["max_rows"].tile[:].bitcast(BF16)[0:48, 0:T])

                def time_mix_draw():
                    later(row, act, rwkv_ready, row)
                    draw("rk", kv[:, 0, :])
                    draw("rv", kv[:, 1, :])
                    draw("rr", er[:])

                def sum_squares(use, n, semaphore):
                    slot = slots[use]
                    slot.filled(act, row, use)
                    for i in range(NB):
                        last = act.activation(sq[:, i, :], slot.tile[:, i * P:(i + 1) * P], ACT.Square,
                                              accum_out=ssum[:, n, i:i + 1])
                    last.then_inc(semaphore, 1)

                def experts_tokens():
                    draw("sum", expertsT[:], slot=SUM)
                    if layer == 0:
                        sum_squares("experts_tok", 1, sumsq_experts)
                    else:
                        slot = back["experts_tok"]
                        slot.filled(act, row, "experts_tok")
                        act.activation(gate_tanh[:], slot.tile[:], ACT.Tanh, scale=0.5).then_inc(gate_ready, 1)

                def exponentials(g, u):
                    if u == 0 and g >= 2:
                        OUT.filled(act, row, ("values", g - 2))
                    slot = back[("exp", g, u)]
                    slot.filled(act, row, ("exp", g, u))
                    act.activation(probs[:, g % 2, u, :], slot.tile[:], ACT.Exp).then_inc(slot.taken, 1)

                def state_exponentials():
                    front["rr"].drawn(act, row, "rr")
                    for n in range(2):
                        act.wait_ge(expo_args, row * 2 + n + 1)
                        act.activation(expo[:, 2 * n:2 * n + 2, :], expo[:, 2 * n:2 * n + 2, :], ACT.Exp)\
                            .then_inc(expo_ready, 1)
                    act.activation(er[:], er[:], ACT.Exp, scale=-1.0).then_inc(expo_ready, 1)

                def ffn_tokens():
                    draw("ffn_sum", ffnT[:], slot=OUT)
                    sum_squares("ffn_tok", 2, sumsq_back)

                def end():
                    if layer == 0:
                        act.wait_ge(pre_ready, row + 1)
                        act.activation(gate[:], pre[:], ACT.Silu).then_inc(gate_ready, 1)
                    act.wait_ge(out_ready, row + 1)
                    act.dma_start(out_rows[row], x_out[:]).then_inc(out_stored, 16)

                if stage == "next":
                    return {}
                if stage == "front":
                    return {"xnT": lambda: draw("xnT", xnT[:, 1:]), "qk": queries_keys, "router": router_exp,
                            "weights": weights, "unit": gate_unit, "v": draw_values, "max_rows": max_rows,
                            "rwkv_proj": time_mix_draw}
                return {"experts_tok": experts_tokens, "exp": exponentials, "time_mix": state_exponentials,
                        "values": lambda g: draw(("values", g), attnU[:, g % 2, :], slot=OUT),
                        "attnT": lambda: draw("attnT", attnT[:]),
                        "oproj": lambda: sum_squares("oproj", 0, sumsq_back), "hT": lambda: draw("hT", hT[:]),
                        "ffn": silu_ffn, "ffn_tok": ffn_tokens, "end": end}

            all_rows(act, steps_of)
            act.wait_ge(out_stored, 16 * B + 16)

        @block.gpsimd
        def _(pool):
            pool.wait_ge(weights_loaded, 16 * len(loads))
            pool.wait_ge(setup_done, 1)

            def steps_of(stage, row):
                link = chain(pool, f"pool_{stage}", pool_step[stage], row)

                def inverse_root(dst, n, src, factor):
                    stand(pool)
                    link(pool.tensor_scalar(root_of[:, n, :], src, factor, EPS, ALU.mult, ALU.add))
                    return pool.tensor_tensor(dst, root_of[:, n, :], minus_half[:], ALU.pow)

                def norm():
                    pool.wait_ge(var_ready, row + 1)
                    inverse_root(rstd[:], 3, meanvar[:, :, 1], 1.0).then_inc(rstd_ready, 1)

                def shifted_mix():
                    front["xnT"].drawn(pool, row, "xnT")
                    later(row, pool, front["rr"].full,
                          (row - 1) * front["rr"].per_row + front["rr"].uses.index("rr") + 1)
                    for n in range(3):
                        stand(pool)
                        pool.tensor_scalar(mix_a[:], xnT[:, 0:T], omix[:, n:n + 1], 0.0, ALU.mult, ALU.add)
                        link(pool.tensor_scalar(mix_b[:], xnT[:, 1:], cols[:, 2 + n:3 + n], 0.0, ALU.mult, ALU.add))
                        pool.tensor_tensor(mix[:, n, :], mix_b[:], mix_a[:], ALU.add).then_inc(mix_ready, 1)
                        pool.wait_ge(mix_ready, row * 3 + n + 1)

                def experts_rms():
                    if layer == 0:
                        pool.wait_ge(sumsq_experts, row + 1)
                        inverse_root(rms[:, 1, :], 1, ssum[:, 1, :], 1.0 / C).then_inc(rms_experts, 1)

                def back_rms(n):
                    pool.wait_ge(sumsq_back, row * 2 + (1, 0, 2)[n])
                    inverse_root(rms[:, n, :], n, ssum[:, n, :], 1.0 / C).then_inc(rms_back, 1)

                if stage == "next":
                    return {"norm": norm}
                if stage == "front":
                    return {"mix": shifted_mix}
                return {"experts_tok": experts_rms, "oproj": lambda: back_rms(0), "ffn_tok": lambda: back_rms(2)}

            all_rows(pool, steps_of)

        @block.vector
        def _(dve):
            for slot in (*front_slots, *back_slots, SUM, OUT):
                dve.sem_inc(slot.taken, 1)
            dve.sem_inc(out_stored, 16)
            dve.memset(K[:], 1.0)
            dve.memset(V[:], 0.0).then_inc(v_cleared, 1)
            dve.wait_ge(v_cleared, 1)
            dve.memset(V[:, :, :, DV:DV + 1], 1.0)
            dve.memset(minus_half[:], -0.5)
            dve.memset(taken[:], 0.0)
            dve.memset(w_parts[:], 0.0)
            dve.memset(max_parts[:], 0.0)
            dve.memset(xnT[:, 0:1], 0.0)
            dve.memset(onesb[:], 1.0)
            if layer == 0:
                dve.memset(o_all[:, 0:1], NEG)
                dve.memset(p_all[:, 0:1], 0.0)
                dve.memset(q_all[:, 0:1], 0.0)
            dve.wait_ge(weights_loaded, 16 * len(loads))
            dve.tensor_copy(identb[:], ident[:])
            for dst, wide in narrow:
                dve.tensor_copy(dst, wide)
            if layer == 0:
                dve.tensor_scalar(omix[:], cols[:, 2:5], -1.0, 1.0, ALU.mult, ALU.add)
                dve.wait_ge(decay_exp, 1)
                last = dve.tensor_scalar(decay[:], decay[:], -1.0, None, ALU.mult)
            else:
                dve.scalar_tensor_tensor(out=q_scale1[:], in0=scale_dims[:, 0:1], scalar=scale[:],
                                         in1=scale_dims[:, 1:2], op0=ALU.mult, op1=ALU.add)
                dve.wait_ge(direction_product, 1)
                last = dve.tensor_copy(wqk4[:].rearrange("p t d -> p (t d)"), front_slots[0].tile[:, 0:64])
            last.then_inc(setup_done, 1)
            dve.wait_ge(setup_done, 1)

            def steps_of(stage, row):
                slots = front if stage == "front" else back
                link = chain(dve, f"dve_{stage}", dve_step[stage], row)

                def layer_norm():
                    dve.wait_ge(x_loaded, row * 16 + 16)
                    for i in range(NB):
                        last = dve.bn_stats(stats[:, i, :], x_in[:, i, :])
                    link(last)
                    stand(dve)
                    for i in range(NB):
                        last = dve.bn_aggr(meanvar[:, i, :], stats[:, i, :])
                    last.then_inc(var_ready, 1)
                    dve.wait_ge(var_ready, row + 1)
                    dve.wait_ge(rstd_ready, row + 1)
                    for i in range(NB):
                        last = dve.tensor_scalar(xn[:, i, :], x_in[:, i, :], meanvar[:, i, 0:1], rstd[:, i:i + 1],
                                                 ALU.subtract, ALU.mult)
                    last.then_inc(xn_ready, 1)

                def split(dst, value, rest, sign=1.0):
                    link(dve.tensor_scalar(dst(0), value, sign, None, ALU.mult))
                    link(dve.scalar_tensor_tensor(out=rest, in0=value, scalar=sign, in1=dst(0),
                                                  op0=ALU.mult, op1=ALU.subtract))
                    link(dve.tensor_copy(dst(1), rest))
                    link(dve.tensor_tensor(rest, rest, dst(1), ALU.subtract))
                    return dve.tensor_copy(dst(2), rest)

                def split_queries():
                    rows = (P, 32)[layer]
                    front["k"].drawn(dve, row, "k")
                    front["q"].drawn(dve, row, "q")
                    split(lambda s: parts[0:rows, :, s, :], compact[0:rows], split_rest[0:rows])\
                        .then_inc(parts_ready, 1)

                lg, pr, ex = logits[:, :, 0:E], pri[:, :, 0:E], expl[:, :, 0:E]

                def wide(col):
                    return top[:, :, col:col + 1].to_broadcast([P, NB, E])

                def router_choice():
                    slot = front["router"]
                    slot.filled(dve, row, "router")
                    dve.tensor_copy(lg, slot.tile[:, 0:NB * E].rearrange("p (i e) -> p i e", e=E)).then_inc(slot.taken, 1)
                    slot.drawn(dve, row, "router")
                    for k in range(2):
                        link(dve.tensor_reduce(top[:, :, 0:1], lg, AX.X, ALU.max))
                        if k == 0:
                            dve.tensor_tensor(ex, lg, wide(0), ALU.subtract).then_inc(logits_shifted, 1)
                        link(dve.tensor_tensor(pr, lg, wide(0), ALU.is_equal))
                        link(dve.tensor_tensor(pr, pr, ramp[:, :, 0:E], ALU.mult))
                        link(dve.tensor_reduce(top[:, :, 1:2], pr, AX.X, ALU.max))
                        link(dve.tensor_tensor(first[:, :, k, 0:E], pr, wide(1), ALU.is_equal))
                        if k == 0:
                            link(dve.scalar_tensor_tensor(out=lg, in0=first[:, :, 0, 0:E], scalar=NEG, in1=lg,
                                                          op0=ALU.mult, op1=ALU.add))
                    if layer == 1:
                        dve.tensor_copy(firstb[:], first[:]).then_inc(choice_ready, 1)
                    dve.wait_ge(expl_ready, row + 1)
                    link(dve.tensor_reduce(top[:, :, 2:3], ex, AX.X, ALU.add))
                    link(dve.reciprocal(top[:, :, 3:4], top[:, :, 2:3]))
                    link(dve.tensor_tensor(ex, ex, wide(3), ALU.mult))
                    if layer == 0:
                        choice_weights()

                def choice_weights():
                    link(dve.tensor_tensor(pr, first[:, :, 0, 0:E], first[:, :, 1, 0:E], ALU.add))
                    link(dve.tensor_tensor(wtop[:, :, 0:E], pr, ex, ALU.mult))
                    split(lambda s: w_parts[:, :, s, 0:E], wtop[:, :, 0:E], w_rest[:, :, 0:E])\
                        .then_inc(w_parts_ready, 1)

                def keep_ranked():
                    slot = front["rank"]
                    slot.filled(dve, row, "rank")
                    taken_row = taken[:].rearrange("p (o k) e -> p o (k e)", o=1)
                    link(dve.tensor_tensor(rank[:].rearrange("p i k e -> p i (k e)"),
                                           slot.tile[:, 0:NB * 32].rearrange("p (i n) -> p i n", i=NB),
                                           taken_row.to_broadcast([P, NB, 32]), ALU.add))
                    dve.tensor_tensor(taken[:].rearrange("p k e -> p (k e)"), slot.tile[:, NB * 32:(NB + 1) * 32],
                                      taken[:].rearrange("p k e -> p (k e)"), ALU.add).then_inc(slot.taken, 1)
                    link(dve.scalar_tensor_tensor(out=first[:].rearrange("p i k e -> p (i k e)"),
                                                  in0=rank[:].rearrange("p i k e -> p (i k e)"), scalar=capacity,
                                                  in1=first[:].rearrange("p i k e -> p (i k e)"),
                                                  op0=ALU.is_lt, op1=ALU.mult))
                    choice_weights()

                def expert_unit(e):
                    gate_slot, up, weight = front[("gate", e)], front[("up", e)], front[("weight", e)]
                    t = gated_e[:, e % LEAD[layer], :]
                    if e < by_tanh:
                        dve.wait_ge(tanh_e_ready, row * by_tanh + e + 1)
                        dve.scalar_tensor_tensor(out=t, in0=t, scalar=1.0, in1=gate_slot.tile[:],
                                                 op0=ALU.add, op1=ALU.mult).then_inc(gate_slot.taken, 1)
                    up.filled(dve, row, ("up", e))
                    gate_slot.drawn(dve, row, ("gate", e))
                    dve.scalar_tensor_tensor(out=t, in0=t, scalar=0.5 if e < by_tanh else 1.0, in1=up.tile[:],
                                             op0=ALU.mult, op1=ALU.mult).then_inc(up.taken, 1)
                    if e >= LEAD[layer]:
                        expert_hidden(e)

                def expert_hidden(e):
                    up, weight = front[("up", e)], front[("weight", e)]
                    if e >= 2:
                        dve.wait_ge(hidden_e_used, row * (E - 1) + e - 1)
                    up.drawn(dve, row, ("up", e))
                    weight.filled(dve, row, ("weight", e))
                    dve.tensor_tensor(hidden_e[:, e % 2, :], gated_e[:, e % LEAD[layer], :], weight.tile[:], ALU.mult)\
                        .then_inc(weight.taken, 1)

                def max_unit(n):
                    i, h0, heads = max_units(H)[n]
                    slot = front[("max", n)]
                    slot.filled(dve, row, ("max", n))
                    src = slot.tile[:].rearrange("p (c k) -> p c k", c=heads)
                    dve.tensor_reduce(row_max[:, i, h0:h0 + heads], src[:, :, 0:(i + 1) * P], AX.X, ALU.max)\
                        .then_inc(slot.taken, 1)

                def max_rows():
                    n = len(max_units(H))
                    for use in [("max", m) for m in range(n - 3, n)]:
                        front[use].drawn(dve, row, use)
                    split(lambda s: max_parts[:, :, s, 0:H], row_max[:, :, 0:H], max_rest[:, :, 0:H], -1.0)\
                        .then_inc(max_parts_ready, 1)

                def rms_scaled(dst, use, n, norm, ready, value):
                    slot = slots[use]
                    slot.filled(dve, row, use)
                    dve.wait_ge(ready, value)
                    for i in range(NB):
                        last = dve.scalar_tensor_tensor(out=dst[:, i, :], in0=slot.tile[:, i * P:(i + 1) * P],
                                                        scalar=rms[:, n, i:i + 1], in1=norms[:, norm, :],
                                                        op0=ALU.mult, op1=ALU.mult)
                    last.then_inc(slot.taken, 1)
                    slot.drawn(dve, row, use)

                def experts_tokens():
                    if layer == 0:
                        rms_scaled(experts, "experts_tok", 1, 2, rms_experts, row + 1)
                    else:
                        slot = back["experts_tok"]
                        dve.wait_ge(gate_ready, row + 1)
                        dve.scalar_tensor_tensor(out=experts[:].rearrange("p i c -> p (i c)"), in0=gate_tanh[:],
                                                 scalar=1.0, in1=slot.tile[:], op0=ALU.add, op1=ALU.mult)\
                            .then_inc(slot.taken, 1)
                        slot.drawn(dve, row, "experts_tok")

                def normalise_attention(g):
                    slot = back[("turn", g)]
                    slot.filled(dve, row, ("turn", g))
                    src = slot.tile[:].rearrange("p (i c d) -> p i c d", i=NB, c=4)
                    if g:
                        back[("turn", g - 1)].drawn(dve, row, ("turn", g - 1))
                    link(dve.reciprocal(rsum[:], src[:, :, :, DV]))
                    dst = attn[:, :, 4 * g * DV:4 * (g + 1) * DV].rearrange("p i (c d) -> p i c d", c=4)
                    dve.tensor_tensor(dst, src[:, :, :, 0:DV], rsum[:].unsqueeze(3).to_broadcast([P, NB, 4, DV]), ALU.mult)\
                        .then_inc(slot.taken, 1)
                    if g == G - 1:
                        slot.drawn(dve, row, ("turn", g))
                        dve.sem_inc(attn_ready, 1)

                def time_mix_states():
                    k, u, w = kv[:, 0, :], cols[:, 1:2], decay[:]
                    o_before, o_now = o_all[:, 0:T], o_all[:, 1:]
                    for use in ("rk", "rv", "rr"):
                        front[use].drawn(dve, row, use)
                    link(dve.tensor_tensor_scan(o_now, w.to_broadcast([P, T]), k, NEG, ALU.add, ALU.max))
                    dve.scalar_tensor_tensor(out=expo[:, 0, :], in0=o_before, scalar=w, in1=o_now,
                                             op0=ALU.add, op1=ALU.subtract)
                    dve.tensor_tensor(expo[:, 1, :], k, o_now, ALU.subtract).then_inc(expo_args, 1)
                    link(dve.scalar_tensor_tensor(out=t1[:], in0=k, scalar=u, in1=o_before, op0=ALU.add, op1=ALU.max))
                    dve.tensor_tensor(expo[:, 2, :], o_before, t1[:], ALU.subtract)
                    dve.scalar_tensor_tensor(out=expo[:, 3, :], in0=k, scalar=u, in1=t1[:],
                                             op0=ALU.add, op1=ALU.subtract).then_inc(expo_args, 1)

                def time_mix_sums():
                    v = kv[:, 1, :]
                    dve.wait_ge(expo_ready, row * 3 + 1)
                    dve.wait_ge(expo_args, row * 2 + 2)
                    link(dve.tensor_tensor(t1[:], expo[:, 1, :], v, ALU.mult))
                    dve.tensor_tensor_scan(q_all[:, 1:], expo[:, 0, :], expo[:, 1, :], 0.0, ALU.mult, ALU.add)
                    link(dve.tensor_tensor_scan(p_all[:, 1:], expo[:, 0, :], t1[:], 0.0, ALU.mult, ALU.add))

                def time_mix_result():
                    v = kv[:, 1, :]
                    dve.wait_ge(expo_ready, row * 3 + 2)
                    dve.tensor_tensor(t2[:], expo[:, 2, :], p_all[:, 0:T], ALU.mult)
                    dve.tensor_tensor(expo[:, 0, :], expo[:, 2, :], q_all[:, 0:T], ALU.mult)
                    link(dve.tensor_tensor(t1[:], expo[:, 3, :], v, ALU.mult))
                    link(dve.tensor_tensor(expo[:, 0, :], expo[:, 0, :], expo[:, 3, :], ALU.add))
                    link(dve.tensor_tensor(t1[:], t1[:], t2[:], ALU.add))

                def time_mix_quotient():
                    dve.wait_ge(expo_ready, row * 3 + 3)
                    link(dve.scalar_tensor_tensor(out=expo[:, 0, :], in0=er[:], scalar=1.0, in1=expo[:, 0, :],
                                                  op0=ALU.add, op1=ALU.mult))
                    link(dve.reciprocal(t2[:], expo[:, 0, :]))
                    dve.tensor_tensor(rwkvT[:], t1[:], t2[:], ALU.mult).then_inc(rwkv_ready, 1)

                def attention_residual():
                    rms_scaled(tok_a, "oproj", 0, 0, rms_back, row * 2 + 1)
                    dve.tensor_tensor(hres[:], tok_a[:], xn_kept[:], ALU.add).then_inc(h_ready, 1)
                    dve.wait_ge(h_ready, row + 1)
                    link(dve.tensor_tensor(pre[:], hres[:], experts[:], ALU.add))

                def ffn_unit(f):
                    gate_slot, up = back[("gate", f)], back[("up", f)]
                    t = hidden_f[:, f % 2, :]
                    up.filled(dve, row, ("up", f))
                    gate_slot.drawn(dve, row, ("gate", f))
                    dve.tensor_tensor(t, t, up.tile[:], ALU.mult).then_inc(up.taken, 1)

                def ffn_tokens():
                    rms_scaled(tok_a, "ffn_tok", 2, 1, rms_back, row * 2 + 2)
                    dve.tensor_tensor(pre[:], pre[:], tok_a[:], ALU.add).then_inc(pre_ready, 1)
                    dve.wait_ge(pre_ready, row + 1)

                def end():
                    if layer == 0:
                        g = gate[:].rearrange("p i c -> p (i c)")
                        dve.wait_ge(gate_ready, row + 1)
                    else:
                        g = experts[:].rearrange("p i c -> p (i c)")
                    slot = back["s"]
                    slot.filled(dve, row, "s")
                    dve.wait_ge(out_stored, row * 16 + 16)
                    dve.scalar_tensor_tensor(out=x_out[:].rearrange("p i c -> p (i c)"), in0=g, scalar=(1.0, 0.5)[layer],
                                             in1=slot.tile[:], op0=ALU.mult, op1=ALU.mult).then_inc(slot.taken, 1)
                    slot.drawn(dve, row, "s")
                    dve.wait_ge(res_loaded, row * 16 + 16)
                    dve.tensor_tensor(x_out[:], x_out[:], x_res[:], ALU.add).then_inc(out_ready, 1)

                if stage == "next":
                    return {"norm": layer_norm}
                if stage == "front":
                    def weights():
                        for e in range(LEAD[layer]):
                            expert_hidden(e)

                    return {**({"keep": lambda: link(dve.tensor_copy(xn_kept[:], xn[:]))} if layer == 0 else {}),
                            "split": split_queries, "router": router_choice, "rank": keep_ranked,
                            "unit": expert_unit, "weights": weights, "max": max_unit, "max_split": max_rows}
                return {"experts_tok": experts_tokens, "states": time_mix_states, "time_mix": time_mix_sums, "time_mix2": time_mix_result,
                        "time_mix3": time_mix_quotient, "turn": normalise_attention,
                        "oproj": attention_residual, "ffn": ffn_unit, "ffn_tok": ffn_tokens, "end": end}

            all_rows(dve, steps_of)


def build(nc, a, out):
    B, T, _ = a["x"].shape
    experts = a["gate_w"].shape[0]
    capacity = float(max(1, -(-(B * T * 2 * 5) // (experts * 4))))
    between = nc.dram_tensor("between", list(a["x"].shape), F32, kind="Internal").ap()
    build_layer(nc, a, 0, a["x"], between, capacity)
    build_layer(nc, a, 1, between, out, capacity)


def shape_constants():
    import itertools

    n = np.arange(P)
    pick = np.zeros((48, 16, P), np.float32)
    for e in range(16):
        pick[[e, 16 + e, 32 + e], e, :] = 1
    dirs = np.array(list(itertools.product([-1.0, 1.0], repeat=3)), dtype=np.float32)
    dirs = dirs / np.linalg.norm(dirs, axis=1, keepdims=True)
    m4 = np.zeros((24, 2, 4, 4), np.float32)
    for h in range(8):
        for d in range(3):
            m4[3 * h + d, h // 4, d, h % 4] = 1
            m4[3 * h + d, h // 4, 3, h % 4] = dirs[h, d]
    scaled = np.tile((np.arange(4) < 3).astype(np.float32).repeat(4), 2)
    return {
        "ident": np.eye(P, dtype=np.float32),
        "future_key": np.where(n[None, :] > n[:, None], NEG, 0).astype(np.float32),
        "past_query": np.where(n[None, :] < n[:, None], NEG, 0).astype(np.float32),
        "earlier": (n[:, None] < n[None, :]).astype(np.float32),
        "pick": pick.reshape(48, 16 * P),
        "ramp": np.broadcast_to(16 - np.arange(16, dtype=np.float32), (P, 4, 16)).copy(),
        "m4": m4.reshape(24, 32),
        "scale_dims": np.stack([scaled, 1 - scaled], 1),
    }


def kernel(**inputs):
    import concourse.bacc as bacc
    from concourse.bass_utils import run_bass_kernel_spmd

    x = {k: np.asarray(v) for k, v in inputs.items()}
    L0, L1 = "L0_attn_", "L1_attn_"

    def by_dim(w):
        return np.ascontiguousarray(w.reshape(P, 2, 8, 8).transpose(0, 1, 3, 2).reshape(P, P))

    arrays = {
        "x": x[L0 + "x"],
        "wq": by_dim(x["L0_ffn_wq"]), "wk": by_dim(x["L0_ffn_wk"]), "wv": x["L0_ffn_wv"], "wo": x["L0_ffn_wo"],
        "rk": x[L0 + "Wk"].T, "rv": x[L0 + "Wv"].T, "rr": x[L0 + "Wr"].T, "ro": x[L0 + "Wo"].T,
        "w1": x["L0_ffn_w1"], "w3": x["L0_ffn_w3"], "w2": x["L0_ffn_w2"],
        "router0": x["L0_ffn_router_w"], "ew1": x["L0_ffn_ew1"], "ew2": x["L0_ffn_ew2"], "ew3": x["L0_ffn_ew3"],
        "Wq1": x[L1 + "Wq"], "Wk1": x[L1 + "Wk"], "v1w": x[L1 + "Wv"].T, "o1w": x[L1 + "Wo"].T,
        "scale": x[L1 + "scale"].reshape(1, 1),
        "router1": x["L1_ffn_router_w"], "gate_w": x["L1_ffn_gate_w"], "up_w": x["L1_ffn_up_w"],
        "down_w": x["L1_ffn_down_w"],
        **{n: x[L0 + n] for n in ("time_decay", "time_first")},
        **{n: x[L0 + n].reshape(P) for n in ("time_mix_k", "time_mix_v", "time_mix_r")},
        **{n: x["L0_ffn_" + n] for n in ("attn_norm_w", "ff_norm_w", "moe_norm_w")},
        **shape_constants(),
    }
    nc = bacc.Bacc("TRN2", target_bir_lowering=False, num_devices=1)
    arrays = {f"in_{k}": np.ascontiguousarray(v) for k, v in arrays.items()}
    args = {k[3:]: nc.dram_tensor(k, v.shape, mybir.dt.from_np(v.dtype), kind="ExternalInput").ap()
            for k, v in arrays.items()}
    out = nc.dram_tensor("out_0", x[L0 + "x"].shape, F32, kind="ExternalOutput").ap()
    build(nc, args, out)
    r = run_bass_kernel_spmd(nc, [arrays], core_ids=[0])
    return r.results[0]["out_0"]
```
